# Optimizing a Trainium2 kernel written in Bass

```python
import numpy as np
import jax
import jax.numpy as jnp

def _softmax(x, axis=-1):
    return jax.nn.softmax(x, axis=axis)

def _gelu(x):
    return jax.nn.gelu(x, approximate=True)

def _silu(x):
    return jax.nn.silu(x)

def _sigmoid(x):
    return jax.nn.sigmoid(x)

def _layernorm(x, axis=-1, eps=1e-05):
    m = jnp.mean(x, axis=axis, keepdims=True)
    v = jnp.var(x, axis=axis, keepdims=True)
    return (x - m) / jnp.sqrt(v + eps)

def _scatter_add(tgt, idx, src, axis=0):
    return tgt.at[idx].add(src)

def _segment_sum(src, seg, n):
    return jax.ops.segment_sum(src, seg, n)
kernel_name = 'mk_adj_resnorm_d2_adj_r2_57f39b'

def setup_inputs(seed: int=0):
    np.random.seed(seed)
    _w = jnp.asarray

    def _rec_inputs():
        import jax
        import jax.numpy as jnp
        _gk = jax.random.key(seed)
        x = -0.000125 + 0.9999 * jax.random.normal(jax.random.fold_in(_gk, 1), (128, 64, 512), jnp.float32)
        _a = jax.random.bernoulli(jax.random.fold_in(_gk, 2), 0.125, (64, 64))
        adj = _a.astype(jnp.int32)
        return (x, adj)
    x, adj = _rec_inputs()

    def _L0_gnn_setup():
        import jax, jax.numpy as jnp
        import numpy as np
        B, N, E, H = (64, 256, 512, 16)
        DH = E // H
        key = jax.random.key(seed)
        ks = jax.random.split(key, 5)
        x = jax.random.normal(ks[0], (B, N, E), dtype=jnp.float32)
        Wqkv = jax.random.normal(ks[1], (E, 3 * E), dtype=jnp.float32) * 0.02
        bqkv = jnp.zeros((3 * E,), dtype=jnp.float32)
        Wproj = jax.random.normal(ks[2], (E, E), dtype=jnp.float32) * 0.02
        bproj = jnp.zeros((E,), dtype=jnp.float32)
        adj = jax.random.randint(ks[3], (N, N), 0, 2, dtype=jnp.int32)
        return {'x': x, 'Wqkv': Wqkv, 'bqkv': bqkv, 'Wproj': Wproj, 'bproj': bproj, 'adj': adj}
    _L0_gnn_all = _L0_gnn_setup()
    _L0_gnn_in = {k: v for k, v in _L0_gnn_all.items() if k in ('Wqkv', 'bqkv', 'Wproj', 'bproj')}
    del _L0_gnn_all

    def _L1_gnn_setup():
        import jax, jax.numpy as jnp
        import numpy as np
        B, N, E, H = (64, 256, 512, 16)
        DH = E // H
        key = jax.random.key(seed)
        ks = jax.random.split(key, 5)
        x = jax.random.normal(ks[0], (B, N, E), dtype=jnp.float32)
        Wqkv = jax.random.normal(ks[1], (E, 3 * E), dtype=jnp.float32) * 0.02
        bqkv = jnp.zeros((3 * E,), dtype=jnp.float32)
        Wproj = jax.random.normal(ks[2], (E, E), dtype=jnp.float32) * 0.02
        bproj = jnp.zeros((E,), dtype=jnp.float32)
        adj = jax.random.randint(ks[3], (N, N), 0, 2, dtype=jnp.int32)
        return {'x': x, 'Wqkv': Wqkv, 'bqkv': bqkv, 'Wproj': Wproj, 'bproj': bproj, 'adj': adj}
    _L1_gnn_all = _L1_gnn_setup()
    _L1_gnn_in = {k: v for k, v in _L1_gnn_all.items() if k in ('Wqkv', 'bqkv', 'Wproj', 'bproj')}
    del _L1_gnn_all
    return {'x': x, 'adj': adj, 'L0_gnn_Wqkv': _L0_gnn_in['Wqkv'], 'L0_gnn_bqkv': _L0_gnn_in['bqkv'], 'L0_gnn_Wproj': _L0_gnn_in['Wproj'], 'L0_gnn_bproj': _L0_gnn_in['bproj'], 'L1_gnn_Wqkv': _L1_gnn_in['Wqkv'], 'L1_gnn_bqkv': _L1_gnn_in['bqkv'], 'L1_gnn_Wproj': _L1_gnn_in['Wproj'], 'L1_gnn_bproj': _L1_gnn_in['bproj']}

def reference(x, adj, L0_gnn_Wqkv, L0_gnn_bqkv, L0_gnn_Wproj, L0_gnn_bproj, L1_gnn_Wqkv, L1_gnn_bqkv, L1_gnn_Wproj, L1_gnn_bproj):
    import jax
    import jax.numpy as jnp

    def _L0_gnn_ref(x, Wqkv, bqkv, Wproj, bproj, adj):
        import jax, jax.numpy as jnp
        import numpy as np
        B, N, E, H = (64, 256, 512, 16)
        DH = E // H
        b, n, e = x.shape
        h, dh = (H, e // H)
        qkv = (x @ Wqkv + bqkv).reshape(b, n, 3, h, dh)
        qkv = jnp.transpose(qkv, (2, 0, 3, 1, 4))
        q, k, v = (qkv[0], qkv[1], qkv[2])
        mask = adj + jnp.eye(n, dtype=adj.dtype) > 0
        scale = 1.0 / jnp.sqrt(jnp.asarray(dh, dtype=x.dtype))
        scores = jnp.einsum('bhnd,bhmd->bhnm', q, k) * scale
        scores = jnp.where(mask[None, None], scores, jnp.finfo(scores.dtype).min)
        attn = jax.nn.softmax(scores, axis=-1)
        y = jnp.einsum('bhnm,bhmd->bhnd', attn, v)
        y = jnp.transpose(y, (0, 2, 1, 3)).reshape(b, n, e)
        return y @ Wproj + bproj

    def _L1_gnn_ref(x, Wqkv, bqkv, Wproj, bproj, adj):
        import jax, jax.numpy as jnp
        import numpy as np
        B, N, E, H = (64, 256, 512, 16)
        DH = E // H
        b, n, e = x.shape
        h, dh = (H, e // H)
        qkv = (x @ Wqkv + bqkv).reshape(b, n, 3, h, dh)
        qkv = jnp.transpose(qkv, (2, 0, 3, 1, 4))
        q, k, v = (qkv[0], qkv[1], qkv[2])
        mask = adj + jnp.eye(n, dtype=adj.dtype) > 0
        scale = 1.0 / jnp.sqrt(jnp.asarray(dh, dtype=x.dtype))
        scores = jnp.einsum('bhnd,bhmd->bhnm', q, k) * scale
        scores = jnp.where(mask[None, None], scores, jnp.finfo(scores.dtype).min)
        attn = jax.nn.softmax(scores, axis=-1)
        y = jnp.einsum('bhnm,bhmd->bhnd', attn, v)
        y = jnp.transpose(y, (0, 2, 1, 3)).reshape(b, n, e)
        return y @ Wproj + bproj
    x = _layernorm(x + _L0_gnn_ref(x, L0_gnn_Wqkv, L0_gnn_bqkv, L0_gnn_Wproj, L0_gnn_bproj, adj), axis=-1)
    x = _layernorm(x + _L1_gnn_ref(x, L1_gnn_Wqkv, L1_gnn_bqkv, L1_gnn_Wproj, L1_gnn_bproj, adj), axis=-1)
    return x

_drawn_inputs = setup_inputs


def setup_inputs(seed=0):
    import zlib

    import numpy as np

    out = dict(_drawn_inputs(seed))
    spreads = {'L0_gnn_bqkv': (0.0, 0.1),
     'L0_gnn_bproj': (0.0, 0.1),
     'L1_gnn_bqkv': (0.0, 0.1),
     'L1_gnn_bproj': (0.0, 0.1)}
    factors = {}
    for name, (base, spread) in spreads.items():
        noise = np.random.default_rng([zlib.crc32(name.encode()), seed]).standard_normal(out[name].shape)
        drawn = base * np.exp(spread * noise) if base else spread * noise
        out[name] = jnp.asarray(drawn.astype(out[name].dtype))
    for name, factor in factors.items():
        out[name] = (out[name] * factor).astype(out[name].dtype)
    return out
```

```python
from contextlib import ExitStack

import concourse.bass as bass
import concourse.mybir as mybir

F32 = mybir.dt.float32
F32R = mybir.dt.float32r
I32 = mybir.dt.int32
ALU = mybir.AluOpType
ACT = mybir.ActivationFunctionType
AX_X = mybir.AxisListType.X

P = 128
NODES = 64
E = 512
HEADS = 16
DH = E // HEADS
TOKENS = 128 * NODES
GROUP = 512
STAGES = TOKENS // GROUP
PAIRS = GROUP // P
KT = E // P
BLK = 4
WCOLS = 4 * E
V0, PROJ0 = 2 * E, 3 * E
LAYER_PAIRS = STAGES * PAIRS
EPS = 1e-5
MASKED = -3.0e38
SCALE = float(DH) ** -0.5
UNITS = 12
LANES = 3


def build(nc, x, adj, weights, out):
    ctx = ExitStack()
    with ctx:
        def sb(name, shape, dt=F32):
            return ctx.enter_context(nc.sbuf_tensor(name, shape, dt))

        def sem(name):
            return ctx.enter_context(nc.semaphore(name))

        hidden = nc.dram_tensor("hidden", [TOKENS, E], F32).ap()

        w_hi = sb("w_hi", [P, KT, WCOLS], F32R)
        w_lo = sb("w_lo", [P, KT, WCOLS], F32R)
        bias_qkv = sb("bias_qkv", [P, 12])
        bias_v_wide = sb("bias_v_wide", [P, KT, P])
        bias_out = sb("bias_out", [P, E])
        x_in = sb("x_in", [P, PAIRS, E])
        x_res = sb("x_res", [P, 2, PAIRS, E])
        xT_hi = sb("xT_hi", [P, KT, GROUP], F32R)
        xT_lo = sb("xT_lo", [P, KT, GROUP], F32R)
        qkT = sb("qkT", [P, 2, 8, GROUP])
        w_raw = qkT[:, 1].rearrange("p (b c) t -> p b (c t)", b=2)
        q_hi = sb("q_hi", [P, BLK, 2, P], F32R)
        q_lo = sb("q_lo", [P, BLK, 2, P], F32R)
        k_hi = sb("k_hi", [P, BLK, 2, 4, NODES], F32R)
        k_lo = sb("k_lo", [P, BLK, 2, 4, NODES], F32R)
        v_sel = sb("v_sel", [P, 2, PAIRS, 2, E // 2])
        probs = sb("probs", [P, 2, HEADS * NODES])
        probsT = sb("probsT", [P, 2 * GROUP])
        yT_hi = sb("yT_hi", [P, 2, 2 * P], F32R)
        yT_lo = sb("yT_lo", [P, 2, 2 * P], F32R)
        normed = sb("normed", [P, PAIRS, E])
        row_max = sb("row_max", [P, HEADS])
        row_sum = sb("row_sum", [P, HEADS])
        row_inv = sb("row_inv", [P, HEADS])
        stats = sb("stats", [P, 6])
        mean_var = sb("mean_var", [P, 2, 2])
        var_eps = sb("var_eps", [P, 1])
        rstd = sb("rstd", [P, 2])
        minus_half = sb("minus_half", [P, 1])
        epsilon = sb("epsilon", [P, 1])
        ident = sb("ident", [P, P])
        eye = sb("eye", [P, NODES])
        adj_in = sb("adj_in", [P, NODES], I32)
        mask = sb("mask", [P, NODES])
        acc = ctx.enter_context(nc.psum_tensor("acc", [P, 4, 512], F32))
        att = ctx.enter_context(nc.psum_tensor("att", [P, 4, 512], F32))

        adj_loaded = sem("adj_loaded")
        x_loaded = sem("x_loaded")
        w_loaded = [sem(f"w_loaded{b}") for b in range(2)]
        bias_loaded = sem("bias_loaded")
        stored = [sem(f"stored{b}") for b in range(PAIRS)]
        bias_mixed = sem("bias_mixed")
        xT_ready = sem("xT_ready")
        unit_ready = [sem(f"unit_ready{i}") for i in range(LANES)]
        scores_ready = sem("scores_ready")
        probsT_ready = sem("probsT_ready")
        yT_ready = sem("yT_ready")
        proj_ready = sem("proj_ready")
        attend_begun = sem("attend_begun")
        w_hi_done = sem("w_hi_done")
        xT_hi_done = sem("xT_hi_done")
        unit_saved = [sem(f"unit_saved{i}") for i in range(LANES)]
        exp_done = sem("exp_done")
        probsT_saved = sem("probsT_saved")
        yT_hi_done = sem("yT_hi_done")
        operands_hi_done = sem("operands_hi_done")
        setup = sem("setup")
        wide_done = sem("wide_done")
        w_lo_done = sem("w_lo_done")
        bias_out_done = sem("bias_out_done")
        xT_lo_done = sem("xT_lo_done")
        masked_done = sem("masked_done")
        max_done = sem("max_done")
        shifted_done = sem("shifted_done")
        sum_done = sem("sum_done")
        inv_done = sem("inv_done")
        probs_done = sem("probs_done")
        yT_lo_done = sem("yT_lo_done")
        operands_lo_done = sem("operands_lo_done")
        residual_done = sem("residual_done")
        stats_done = sem("stats_done")
        mean_var_done = sem("mean_var_done")
        aggregate_begun = sem("aggregate_begun")
        normed_done = sem("normed_done")
        zeroed = sem("zeroed")
        operands_zeroed = sem("operands_zeroed")
        consts_done = sem("consts_done")
        x_res_done = sem("x_res_done")
        var_eps_done = sem("var_eps_done")
        rstd_done = sem("rstd_done")

        block = ctx.enter_context(nc.Block())

        def unit_place(u):
            return u % LANES, u // LANES

        def operand_places(q, k, par, p):
            tok = slice(P * p, P * (p + 1))
            yield (q[:].rearrange("p c b (g t) -> p c (b g) t", g=2)[:, :, 0:4:3, :],
                   qkT[:, par, 0:BLK, tok].rearrange("p c (b t) -> p c b t", b=2))
            for a in range(4):
                rows = slice(DH * a, DH * (a + 1))
                yield k[rows, :, :, a, :], qkT[rows, par, BLK:2 * BLK, tok].rearrange("p c (b t) -> p c b t", b=2)

        def stages(eng, stage):
            stage(0, 0, True, False)
            with eng.Fori(PAIRS, LAYER_PAIRS - 3 * PAIRS + 1, 2 * PAIRS) as n:
                stage(n, 1, False, False)
                stage(n + PAIRS, 0, False, False)
            stage(LAYER_PAIRS - PAIRS, 1, False, True)

        @block.sync
        def _(sp):
            for b in (2, 3):
                sp.sem_inc(stored[b], 16)
            for half in range(2):
                sp.dma_start(adj_in[NODES * half:NODES * (half + 1), :], adj).then_inc(adj_loaded, 16)
            for layer in range(2):
                BASE = layer * LAYER_PAIRS
                wqkv, bqkv, wproj, bproj = weights[layer]
                src = (x if layer == 0 else hidden).rearrange("(t p) e -> p t e", p=P)
                dst = (hidden if layer == 0 else out).rearrange("(t p) e -> p t e", p=P)

                def load_weights(kt):
                    rows = slice(P * kt, P * (kt + 1))
                    sp.dma_start(w_raw[:, kt % 2, 0:PROJ0], wqkv[rows, :]).then_inc(w_loaded[kt % 2], 16)
                    sp.dma_start(w_raw[:, kt % 2, PROJ0:WCOLS], wproj[rows, :]).then_inc(w_loaded[kt % 2], 16)

                if layer:
                    for b in range(PAIRS):
                        sp.wait_ge(stored[b], 16 * STAGES + 16 * (b // 2))
                sp.dma_start(x_in[:], src[:, 0:PAIRS, :]).then_inc(x_loaded, 16)
                load_weights(0)
                load_weights(1)
                sp.dma_start(bias_qkv[:], bqkv).then_inc(bias_loaded, 16)
                sp.dma_start(bias_out[:], bproj.partition_broadcast(P)).then_inc(bias_loaded, 16)
                for kt in (2, 3):
                    sp.wait_ge(w_lo_done, 4 * layer + kt - 1)
                    sp.wait_ge(bias_mixed, 4 * layer + kt - 1)
                    load_weights(kt)
                sp.wait_ge(xT_ready, BASE + PAIRS)
                sp.wait_ge(x_res_done, BASE + PAIRS)
                sp.dma_start(x_in[:], src[:, PAIRS:2 * PAIRS, :]).then_inc(x_loaded, 16)

                def stage(n, par, first, last):
                    for p in range(PAIRS):
                        if not (first and p < 2):
                            sp.wait_ge(normed_done, BASE + n + p - 1)
                            sp.dma_start(dst[:, bass.ds(n + p - 2, 1), :],
                                         normed[:, (p + 2) % 4:(p + 2) % 4 + 1, :]).then_inc(stored[(p + 2) % 4], 16)
                        if p == 3 and not last:
                            sp.wait_ge(xT_ready, BASE + n + 2 * PAIRS)
                            sp.wait_ge(x_res_done, BASE + n + 2 * PAIRS)
                            sp.dma_start(x_in[:], src[:, bass.ds(n + 2 * PAIRS, PAIRS), :]).then_inc(x_loaded, 16)

                stage(0, 0, True, False)
                with sp.Fori(PAIRS, LAYER_PAIRS - 5 * PAIRS + 1, 2 * PAIRS) as n:
                    stage(n, 1, False, False)
                    stage(n + PAIRS, 0, False, False)
                stage(LAYER_PAIRS - 3 * PAIRS, 1, False, False)
                stage(LAYER_PAIRS - 2 * PAIRS, 0, False, True)
                stage(LAYER_PAIRS - PAIRS, 1, False, True)
                for pair in (LAYER_PAIRS - 2, LAYER_PAIRS - 1):
                    sp.wait_ge(normed_done, BASE + pair + 1)
                    sp.dma_start(dst[:, pair:pair + 1, :],
                                 normed[:, pair % 4:pair % 4 + 1, :]).then_inc(stored[pair % 4], 16)
            for b in range(PAIRS):
                sp.wait_ge(stored[b], 2 * 16 * STAGES + 16 * (b // 2))

        @block.tensor
        def _(pe):
            def transpose_x(n, BASE):
                pe.wait_ge(x_loaded, 4 * (BASE + n) + 16)
                for i in range(LANES):
                    pe.wait_ge(unit_saved[i], BASE + n)
                for ft in range(KT):
                    for t in range(PAIRS):
                        last = nc.tensor.transpose(acc[:, ft, P * t:P * (t + 1)],
                                                   x_in[:, t, P * ft:P * (ft + 1)], ident[:])
                    last.then_inc(xT_ready, 1)

            def unit(u, n, BASE):
                lane, turn = unit_place(u)
                if turn == 0:
                    pe.wait_ge(xT_lo_done, BASE + n + PAIRS)
                else:
                    pe.wait_ge(unit_saved[lane], BASE + n + turn)
                for kt in range(KT):
                    for i, (w, xt) in enumerate(((w_hi, xT_hi), (w_hi, xT_lo), (w_lo, xT_hi))):
                        if u < 8:
                            fixed, moving = w[:, kt, P * u:P * (u + 1)], xt[:, kt, :]
                        else:
                            fixed, moving = xt[:, kt, P * (u - 8):P * (u - 7)], w[:, kt, V0:PROJ0]
                        last = nc.tensor.matmul(acc[:, lane, :], fixed, moving,
                                                start=(kt == 0 and i == 0), stop=(kt == KT - 1 and i == 2))
                last.then_inc(unit_ready[lane], 1)

            def scores(n, p, BASE):
                pe.wait_ge(operands_lo_done, BASE + n + p + 1)
                for blk in range(BLK):
                    cols = slice(256 * (blk % 2), 256 * (blk % 2 + 1))
                    for b in range(2):
                        for i, (q, k) in enumerate(((q_hi, k_hi), (q_hi, k_lo), (q_lo, k_hi))):
                            last = nc.tensor.matmul(att[:, blk // 2, cols], q[:, blk, b, :],
                                                    k[:, blk, b, :, :].rearrange("p a m -> p (a m)"),
                                                    start=(b == 0 and i == 0), stop=(b == 1 and i == 2))
                last.then_inc(scores_ready, 1)

            def transpose_probs(n, p, BASE):
                pe.wait_ge(probs_done, BASE + n + p)
                for t in range(8):
                    last = nc.tensor.transpose(att[:, 2 + t // 4, P * (t % 4):P * (t % 4 + 1)],
                                               probs[:, (p + 1) % 2, P * t:P * (t + 1)], ident[:])
                last.then_inc(probsT_ready, 1)

            def attend(n, p, par, drained, BASE):
                q = (p + 3) % 4
                vpar = par if p else 1 - par
                if drained:
                    pe.wait_ge(masked_done, BASE + n + p + 1)
                if p == 1:
                    for i in range(LANES):
                        pe.wait_ge(unit_saved[i], BASE + n + PAIRS)
                pe.wait_ge(probsT_saved, BASE + n + p).then_inc(attend_begun, 1)
                for a in range(4):
                    for j in range(2):
                        for s in range(2):
                            rows = slice(NODES * s, NODES * (s + 1))
                            for b in range(2):
                                last = nc.tensor.matmul(
                                    att[DH * a:DH * (a + 1), s, P * j + NODES * b:P * j + NODES * (b + 1)],
                                    v_sel[rows, vpar, q, b, P * j + DH * a:P * j + DH * (a + 1)],
                                    probsT[rows, P * (2 * a + j) + NODES * b:P * (2 * a + j) + NODES * (b + 1)],
                                    start=True, stop=True)
                last.then_inc(yT_ready, 1)

            def project(n, p, BASE, after_pair):
                pe.wait_ge(yT_lo_done, BASE + n + p)
                if after_pair:
                    pe.wait_ge(residual_done, BASE + n + p - 1)
                for blk in range(BLK):
                    for i, (w, yt) in enumerate(((w_hi, yT_hi), (w_lo, yT_hi), (w_hi, yT_lo))):
                        last = nc.tensor.matmul(acc[:, 3, :], yt[:, blk % 2, P * (blk // 2):P * (blk // 2 + 1)],
                                                w[:, blk, PROJ0:WCOLS],
                                                start=(blk == 0 and i == 0), stop=(blk == BLK - 1 and i == 2))
                last.then_inc(proj_ready, 1)

            pe.wait_ge(consts_done, 5)
            for layer in range(2):
                BASE = layer * LAYER_PAIRS
                pe.wait_ge(wide_done, layer + 1)
                if layer:
                    pe.wait_ge(residual_done, BASE)
                for kt in range(KT):
                    pe.wait_ge(w_loaded[kt % 2], 32 * (2 * layer + kt // 2 + 1))
                    nc.tensor.matmul(acc[:, 3, :], bias_v_wide[:, kt, :], w_raw[:, kt % 2, PROJ0:WCOLS],
                                     start=(kt == 0), stop=(kt == KT - 1)).then_inc(bias_mixed, 1)
                pe.wait_ge(bias_out_done, layer + 1)
                transpose_x(0, BASE)
                pe.wait_ge(w_lo_done, 4 * (layer + 1))
                for u in range(UNITS):
                    unit(u, 0, BASE)

                def stage(n, par, first, last):
                    if not last:
                        if not first:
                            pe.wait_ge(residual_done, BASE + n - 1)
                        transpose_x(n + PAIRS, BASE)
                    for p in range(PAIRS):
                        before = not (first and p == 0)
                        scores(n, p, BASE)
                        if not last:
                            unit(3 * p, n + PAIRS, BASE)
                        if before:
                            transpose_probs(n, p, BASE)
                        if not last:
                            unit(3 * p + 1, n + PAIRS, BASE)
                        if before:
                            attend(n, p, par, True, BASE)
                        if not last:
                            unit(3 * p + 2, n + PAIRS, BASE)
                        if before:
                            project(n, p, BASE, not (first and p == 1))

                stages(pe, stage)
                transpose_probs(LAYER_PAIRS, 0, BASE)
                attend(LAYER_PAIRS, 0, 0, False, BASE)
                project(LAYER_PAIRS, 0, BASE, True)

        @block.scalar
        def _(act):
            def split_x(n, BASE):
                for ft in range(KT):
                    act.wait_ge(xT_ready, BASE + n + ft + 1)
                    nc.scalar.activation(xT_hi[:, ft, :], acc[:, ft, :], ACT.Copy).then_inc(xT_hi_done, 1)

            def save(u, n, par, BASE):
                lane, turn = unit_place(u)
                act.wait_ge(unit_ready[lane], BASE + n + turn + 1)
                if u < 8:
                    nc.scalar.activation(qkT[:, par, u, :], acc[:, lane, :], ACT.Identity,
                                         bias=bias_qkv[:, u:u + 1]).then_inc(unit_saved[lane], 1)
                    return
                for b in range(2):
                    for s in range(2):
                        src = acc[NODES * b:NODES * (b + 1), lane, :].rearrange("t (j s c) -> t s j c", j=2, s=2)
                        dst = v_sel[NODES * s:NODES * (s + 1), par, u - 8, b, :].rearrange("t (j c) -> t j c", j=2)
                        last = nc.scalar.activation(dst, src[:, s, :, :], ACT.Copy)
                last.then_inc(unit_saved[lane], 1)

            def operands_hi(n, p, par, BASE, free):
                if p == 0:
                    act.wait_ge(unit_saved[0], BASE + n + 3)
                    act.wait_ge(unit_saved[1], BASE + n + 3)
                    act.wait_ge(unit_saved[2], BASE + n + 2)
                if free:
                    act.wait_ge(scores_ready, BASE + n + p)
                for dst, src in operand_places(q_hi, k_hi, par, p):
                    last = nc.scalar.activation(dst, src, ACT.Copy)
                last.then_inc(operands_hi_done, 1)

            def save_probsT(n, p, BASE):
                act.wait_ge(probsT_ready, BASE + n + p)
                nc.scalar.activation(probsT[:].rearrange("t (b c) -> t b c", b=2), att[:, 2:4, :],
                                     ACT.Copy).then_inc(probsT_saved, 1)

            def split_y(n, p, BASE):
                act.wait_ge(yT_ready, BASE + n + p)
                nc.scalar.activation(yT_hi[:], att[:, 0:2, 0:2 * P], ACT.Copy).then_inc(yT_hi_done, 1)

            act.wait_ge(operands_zeroed, 4)
            for layer in range(2):
                BASE = layer * LAYER_PAIRS
                if layer:
                    act.wait_ge(proj_ready, BASE)
                for kt in range(KT):
                    act.wait_ge(w_loaded[kt % 2], 32 * (2 * layer + kt // 2 + 1))
                    nc.scalar.activation(w_hi[:, kt, :], w_raw[:, kt % 2, :], ACT.Copy).then_inc(w_hi_done, 1)
                act.wait_ge(bias_loaded, 32 * (layer + 1))
                split_x(0, BASE)
                for u in range(UNITS):
                    save(u, 0, 0, BASE)
                    if u == 7:
                        operands_hi(0, 0, 0, BASE, layer > 0)

                def stage(n, par, first, last):
                    if not last:
                        split_x(n + PAIRS, BASE)
                    for p in range(PAIRS):
                        before = not (first and p == 0)
                        if p < 3:
                            operands_hi(n, p + 1, par, BASE, True)
                        elif not last:
                            operands_hi(n + PAIRS, 0, 1 - par, BASE, True)
                        if not last:
                            save(3 * p, n + PAIRS, 1 - par, BASE)
                        if before:
                            save_probsT(n, p, BASE)
                        act.wait_ge(shifted_done, BASE + n + p + 1)
                        nc.scalar.activation(probs[:, p % 2, :], probs[:, p % 2, :], ACT.Exp,
                                             scale=SCALE).then_inc(exp_done, 1)
                        if not last:
                            save(3 * p + 1, n + PAIRS, 1 - par, BASE)
                        if before:
                            split_y(n, p, BASE)
                        if not last:
                            save(3 * p + 2, n + PAIRS, 1 - par, BASE)

                stages(act, stage)
                save_probsT(LAYER_PAIRS, 0, BASE)
                split_y(LAYER_PAIRS, 0, BASE)

        @block.vector
        def _(dve):
            dve.wait_ge(adj_loaded, 32)
            dve.wait_ge(consts_done, 5)
            nc.vector.tensor_tensor(mask[:], adj_in[:], eye[:], ALU.add).then_inc(setup, 1)
            dve.wait_ge(setup, 1)
            nc.vector.tensor_scalar(mask[:], mask[:], 0.0, 1.0, ALU.is_gt, ALU.subtract).then_inc(setup, 1)
            dve.wait_ge(setup, 2)
            nc.vector.tensor_scalar(mask[:], mask[:], -MASKED, None, ALU.mult).then_inc(setup, 1)
            dve.wait_ge(setup, 3)

            def by_head(ap):
                return ap.unsqueeze(2).broadcast_to([P, HEADS, NODES])

            def split_x(n, BASE):
                for ft in range(KT):
                    dve.wait_ge(xT_hi_done, BASE + n + ft + 1)
                    nc.vector.tensor_tensor(xT_lo[:, ft, :], acc[:, ft, :], xT_hi[:, ft, :].bitcast(F32),
                                            ALU.subtract).then_inc(xT_lo_done, 1)

            def shift_scores(n, p, BASE):
                heads = probs[:, p % 2, :].rearrange("t (h m) -> t h m", h=HEADS)
                dve.wait_ge(scores_ready, BASE + n + p + 1)
                nc.vector.tensor_tensor(
                    probs[:, p % 2, :].rearrange("t (a b m) -> t b a m", a=4, b=BLK),
                    att[:, 0:2, :].rearrange("t g (b a m) -> t (g b) a m", a=4, b=2),
                    mask[:].unsqueeze(1).unsqueeze(1).broadcast_to([P, BLK, 4, NODES]),
                    ALU.add).then_inc(masked_done, 1)
                dve.wait_ge(masked_done, BASE + n + p + 1)
                nc.vector.tensor_reduce(row_max[:], heads, AX_X, ALU.max).then_inc(max_done, 1)
                dve.wait_ge(max_done, BASE + n + p + 1)
                nc.vector.tensor_tensor(heads, heads, by_head(row_max[:]), ALU.subtract).then_inc(shifted_done, 1)

            def operands_lo(n, p, par, BASE):
                dve.wait_ge(operands_hi_done, BASE + n + p + 1)
                for (dst, src), (hi, _) in zip(operand_places(q_lo, k_lo, par, p), operand_places(q_hi, k_hi, par, p)):
                    last = nc.vector.tensor_tensor(dst, src, hi.bitcast(F32), ALU.subtract)
                last.then_inc(operands_lo_done, 1)

            def normalise_probs(n, p, BASE):
                heads = probs[:, p % 2, :].rearrange("t (h m) -> t h m", h=HEADS)
                dve.wait_ge(exp_done, BASE + n + p + 1)
                nc.vector.tensor_reduce(row_sum[:], heads, AX_X, ALU.add).then_inc(sum_done, 1)
                dve.wait_ge(sum_done, BASE + n + p + 1)
                nc.vector.reciprocal(row_inv[:], row_sum[:]).then_inc(inv_done, 1)
                dve.wait_ge(inv_done, BASE + n + p + 1)
                nc.vector.tensor_tensor(heads, heads, by_head(row_inv[:]), ALU.mult).then_inc(probs_done, 1)

            def split_y(n, p, BASE):
                dve.wait_ge(yT_hi_done, BASE + n + p)
                nc.vector.tensor_tensor(yT_lo[:], att[:, 0:2, 0:2 * P], yT_hi[:].bitcast(F32),
                                        ALU.subtract).then_inc(yT_lo_done, 1)

            def residual(n, p, par, BASE):
                q = (p + 3) % 4
                rpar = par if p else 1 - par
                dve.wait_ge(proj_ready, BASE + n + p)
                dve.wait_ge(x_res_done, BASE + n + p)
                nc.vector.tensor_tensor(x_res[:, rpar, q, :], acc[:, 3, :], x_res[:, rpar, q, :],
                                        ALU.add).then_inc(residual_done, 1)
                dve.wait_ge(residual_done, BASE + n + p)
                nc.vector.bn_stats(stats[:], x_res[:, rpar, q, :]).then_inc(stats_done, 1)
                dve.wait_ge(stats_done, BASE + n + p).then_inc(aggregate_begun, 1)
                nc.vector.bn_aggr(mean_var[:, q % 2, :], stats[:]).then_inc(mean_var_done, 1)

            def normalise(n, p, par, BASE, stored_before):
                q = (p + 2) % 4
                rpar = par if p > 1 else 1 - par
                dve.wait_ge(rstd_done, BASE + n + p - 1)
                if stored_before:
                    dve.wait_ge(stored[q], 4 * (BASE + n))
                nc.vector.tensor_scalar(normed[:, q, :], x_res[:, rpar, q, :], mean_var[:, q % 2, 0:1],
                                        rstd[:, q % 2:q % 2 + 1], ALU.subtract, ALU.mult).then_inc(normed_done, 1)

            for layer in range(2):
                BASE = layer * LAYER_PAIRS
                dve.wait_ge(bias_loaded, 32 * (layer + 1))
                nc.vector.tensor_copy(bias_v_wide[:], bias_qkv[:, 8:12].unsqueeze(2).broadcast_to([P, KT, P])).then_inc(wide_done, 1)
                for kt in range(KT):
                    dve.wait_ge(w_hi_done, 4 * layer + kt + 1)
                    nc.vector.tensor_tensor(w_lo[:, kt, :], w_raw[:, kt % 2, :], w_hi[:, kt, :].bitcast(F32),
                                            ALU.subtract).then_inc(w_lo_done, 1)
                dve.wait_ge(bias_mixed, 4 * (layer + 1))
                nc.vector.tensor_tensor(bias_out[:], acc[:, 3, :], bias_out[:], ALU.add).then_inc(bias_out_done, 1)
                split_x(0, BASE)
                operands_lo(0, 0, 0, BASE)

                def stage(n, par, first, last):
                    if not last:
                        split_x(n + PAIRS, BASE)
                    for p in range(PAIRS):
                        shift_scores(n, p, BASE)
                        if not (first and p < 2):
                            normalise(n, p, par, BASE, not (first and layer == 0))
                        if p < 3:
                            operands_lo(n, p + 1, par, BASE)
                        elif not last:
                            operands_lo(n + PAIRS, 0, 1 - par, BASE)
                        normalise_probs(n, p, BASE)
                        if not (first and p == 0):
                            split_y(n, p, BASE)
                            residual(n, p, par, BASE)

                stages(dve, stage)
                normalise(LAYER_PAIRS, 0, 0, BASE, True)
                split_y(LAYER_PAIRS, 0, BASE)
                residual(LAYER_PAIRS, 0, 0, BASE)
                normalise(LAYER_PAIRS, 1, 0, BASE, True)

        @block.gpsimd
        def _(pool):
            nc.gpsimd.memset(ident[:], 0.0).then_inc(zeroed, 1)
            nc.gpsimd.memset(eye[:], 0.0).then_inc(zeroed, 1)
            for t in (q_hi, q_lo, k_hi, k_lo):
                nc.gpsimd.memset(t[:].bitcast(F32), 0.0).then_inc(operands_zeroed, 1)
            nc.gpsimd.memset(minus_half[:], -0.5).then_inc(consts_done, 1)
            nc.gpsimd.memset(epsilon[:], EPS).then_inc(consts_done, 1)
            pool.wait_ge(zeroed, 2)
            nc.gpsimd.affine_select(out=ident[:], in_=ident[:], compare_op=ALU.not_equal, fill=1.0, base=0,
                                    pattern=[[-1, P]], channel_multiplier=1).then_inc(consts_done, 1)
            nc.gpsimd.affine_select(out=eye[:], in_=eye[:], compare_op=ALU.not_equal, fill=1.0, base=0,
                                    pattern=[[-1, NODES]], channel_multiplier=1).then_inc(consts_done, 1)
            pool.wait_ge(consts_done, 4)
            nc.gpsimd.affine_select(out=eye[:], in_=eye[:], compare_op=ALU.not_equal, fill=1.0, base=-NODES,
                                    pattern=[[-1, NODES]], channel_multiplier=1).then_inc(consts_done, 1)

            def add_bias(n, par, BASE, used_before):
                pool.wait_ge(x_loaded, 4 * (BASE + n) + 16)
                for t in range(PAIRS):
                    if used_before:
                        pool.wait_ge(normed_done, BASE + n + t + 1 - 2 * PAIRS)
                    nc.gpsimd.tensor_tensor(x_res[:, par, t, :], x_in[:, t, :], bias_out[:], ALU.add).then_inc(x_res_done, 1)

            def inverse_deviation(n, p, BASE):
                q = (p + 3) % 2
                pool.wait_ge(mean_var_done, BASE + n + p)
                nc.gpsimd.tensor_tensor(var_eps[:], mean_var[:, q, 1:2], epsilon[:], ALU.add).then_inc(var_eps_done, 1)
                pool.wait_ge(var_eps_done, BASE + n + p)
                nc.gpsimd.tensor_tensor(rstd[:, q:q + 1], var_eps[:], minus_half[:], ALU.pow).then_inc(rstd_done, 1)

            for layer in range(2):
                BASE = layer * LAYER_PAIRS
                pool.wait_ge(bias_out_done, layer + 1)
                add_bias(0, 0, BASE, layer > 0)

                def stage(n, par, first, last):
                    for p in range(PAIRS):
                        if p == 2 and not last:
                            add_bias(n + PAIRS, 1 - par, BASE, not first or layer > 0)
                        if not (first and p == 0):
                            inverse_deviation(n, p, BASE)

                stages(pool, stage)
                inverse_deviation(LAYER_PAIRS, 0, BASE)


_WEIGHTS = ["Wqkv", "bqkv", "Wproj", "bproj"]


def kernel(**inputs):
    import numpy as _np
    import concourse.bacc as _bacc
    from concourse import mybir as _mybir
    from concourse.bass_utils import run_bass_kernel_spmd as _run

    nc = _bacc.Bacc("TRN2", target_bir_lowering=False, num_devices=1)
    arrays = {}

    def given(name, shape=None):
        a = _np.asarray(inputs[name])
        a = a.reshape(shape) if shape else a
        if name.endswith("bqkv"):
            a = a.reshape(-1, P).T
        a = _np.ascontiguousarray(a)
        arrays[f"in_{name}"] = a
        return nc.dram_tensor(f"in_{name}", a.shape, _mybir.dt.from_np(a.dtype), kind="ExternalInput").ap()

    x = given("x", (TOKENS, E))
    adj = given("adj")
    weights = [[given(f"L{layer}_gnn_{w}") for w in _WEIGHTS] for layer in range(2)]
    out = nc.dram_tensor("out", (TOKENS, E), F32, kind="ExternalOutput").ap()
    build(nc, x, adj, weights, out)
    r = _run(nc, [arrays], core_ids=[0])
    return _np.asarray(r.results[0]["out"]).reshape(inputs["x"].shape)
```

```python
from contextlib import ExitStack

import concourse.bass as bass
import concourse.mybir as mybir

F32 = mybir.dt.float32
F32R = mybir.dt.float32r
I32 = mybir.dt.int32
ALU = mybir.AluOpType
ACT = mybir.ActivationFunctionType
AX_X = mybir.AxisListType.X

P = 128
NODES = 64
E = 512
HEADS = 16
DH = E // HEADS
TOKENS = 128 * NODES
GROUP = 512
STAGES = TOKENS // GROUP
PAIRS = GROUP // P
KT = E // P
BLK = 4
WCOLS = 4 * E
V0, PROJ0 = 2 * E, 3 * E
PARTS = WCOLS // E
LAYER_PAIRS = STAGES * PAIRS
ALL_PAIRS = 2 * LAYER_PAIRS
BEFORE, FIRST, REFRESH_QK, REFRESH_V, REFRESH_PROJ, LAST = -1, 0, STAGES - 2, STAGES - 1, STAGES, 2 * STAGES - 1
REFRESHED = {(REFRESH_QK, 2): 0, (REFRESH_QK, 3): 1, (REFRESH_V, 0): 2}
LOADED = {(REFRESH_QK, 3): 1, (REFRESH_V, 0): 2, (REFRESH_V, 1): 3}
EPS = 1e-5
MASKED = -3.0e38
SCALE = float(DH) ** -0.5
UNITS = 12
LANES = 3


def build(nc, x, adj, weights, out):
    ctx = ExitStack()
    with ctx:
        def sb(name, shape, dt=F32):
            return ctx.enter_context(nc.sbuf_tensor(name, shape, dt))

        def sem(name):
            return ctx.enter_context(nc.semaphore(name))

        hidden = nc.dram_tensor("hidden", [TOKENS, E], F32).ap()

        w_hi = sb("w_hi", [P, KT, WCOLS], F32R)
        w_lo = sb("w_lo", [P, KT, WCOLS], F32R)
        w_raw = sb("w_raw", [P, KT, E])
        bias_qkv = sb("bias_qkv", [P, 2, 12])
        bias_v_wide = sb("bias_v_wide", [P, KT, P])
        bias_out = sb("bias_out", [P, E])
        x_in = sb("x_in", [P, PAIRS, E])
        x_res = sb("x_res", [P, 2, PAIRS, E])
        xT_hi = sb("xT_hi", [P, KT, GROUP], F32R)
        xT_lo = sb("xT_lo", [P, KT, GROUP], F32R)
        qkT = sb("qkT", [P, 2, 8, GROUP])
        w_raw_kv = qkT[:, 1].rearrange("p (i kt) t -> p i kt t", i=2)
        q_hi = sb("q_hi", [P, BLK, 2, P], F32R)
        q_lo = sb("q_lo", [P, BLK, 2, P], F32R)
        k_hi = sb("k_hi", [P, BLK, 2, 4, NODES], F32R)
        k_lo = sb("k_lo", [P, BLK, 2, 4, NODES], F32R)
        v_sel = sb("v_sel", [P, 2, PAIRS, 2, E // 2])
        probs = sb("probs", [P, 2, HEADS * NODES])
        probsT = sb("probsT", [P, 2 * GROUP])
        yT_hi = sb("yT_hi", [P, 2, 2 * P], F32R)
        yT_lo = sb("yT_lo", [P, 2, 2 * P], F32R)
        row_max = sb("row_max", [P, HEADS])
        row_sum = sb("row_sum", [P, HEADS])
        row_inv = sb("row_inv", [P, HEADS])
        stats = sb("stats", [P, 6])
        mean_var = sb("mean_var", [P, 2, 2])
        var_eps = sb("var_eps", [P, 1])
        rstd = sb("rstd", [P, 2])
        minus_half = sb("minus_half", [P, 1])
        epsilon = sb("epsilon", [P, 1])
        ident = sb("ident", [P, P])
        eye = sb("eye", [P, NODES])
        adj_in = sb("adj_in", [P, NODES], I32)
        mask = sb("mask", [P, NODES])
        acc = ctx.enter_context(nc.psum_tensor("acc", [P, 4, 512], F32))
        att = ctx.enter_context(nc.psum_tensor("att", [P, 4, 512], F32))

        adj_loaded = sem("adj_loaded")
        x_loaded = sem("x_loaded")
        w_loaded = [sem(f"w_loaded{part}") for part in range(PARTS)]
        bias_loaded = sem("bias_loaded")
        bproj_loaded = sem("bproj_loaded")
        stored = [sem(f"stored{b}") for b in range(PAIRS)]
        store_begun = sem("store_begun")
        bias_mixed = sem("bias_mixed")
        xT_ready = sem("xT_ready")
        unit_ready = [sem(f"unit_ready{i}") for i in range(LANES)]
        scores_ready = sem("scores_ready")
        probsT_ready = sem("probsT_ready")
        yT_ready = sem("yT_ready")
        proj_ready = sem("proj_ready")
        attend_begun = sem("attend_begun")
        w_hi_done = sem("w_hi_done")
        xT_hi_done = sem("xT_hi_done")
        unit_saved = [sem(f"unit_saved{i}") for i in range(LANES)]
        exp_done = sem("exp_done")
        probsT_saved = sem("probsT_saved")
        yT_hi_done = sem("yT_hi_done")
        operands_hi_done = sem("operands_hi_done")
        setup = sem("setup")
        wide_done = sem("wide_done")
        w_lo_done = sem("w_lo_done")
        bias_out_done = sem("bias_out_done")
        xT_lo_done = sem("xT_lo_done")
        masked_done = sem("masked_done")
        max_done = sem("max_done")
        shifted_done = sem("shifted_done")
        sum_done = sem("sum_done")
        inv_done = sem("inv_done")
        probs_done = sem("probs_done")
        yT_lo_done = sem("yT_lo_done")
        operands_lo_done = sem("operands_lo_done")
        residual_done = sem("residual_done")
        stats_done = sem("stats_done")
        mean_var_done = sem("mean_var_done")
        aggregate_begun = sem("aggregate_begun")
        normed_done = sem("normed_done")
        zeroed = sem("zeroed")
        operands_zeroed = sem("operands_zeroed")
        consts_done = sem("consts_done")
        x_res_done = sem("x_res_done")
        var_eps_done = sem("var_eps_done")
        rstd_done = sem("rstd_done")

        block = ctx.enter_context(nc.Block())

        def unit_place(u):
            return u % LANES, u // LANES

        def operand_places(q, k, par, p):
            tok = slice(P * p, P * (p + 1))
            yield (q[:].rearrange("p c b (g t) -> p c (b g) t", g=2)[:, :, 0:4:3, :],
                   qkT[:, par, 0:BLK, tok].rearrange("p c (b t) -> p c b t", b=2))
            for a in range(4):
                rows = slice(DH * a, DH * (a + 1))
                yield k[rows, :, :, a, :], qkT[rows, par, BLK:2 * BLK, tok].rearrange("p c (b t) -> p c b t", b=2)

        def stages(eng, stage):
            def alone(k):
                stage(PAIRS * k, k % 2, int(k >= STAGES), k)

            def loop(k, end, layer):
                with eng.Fori(PAIRS * k, PAIRS * (end - 2) + 1, 2 * PAIRS) as n:
                    stage(n, 1, layer, None)
                    stage(n + PAIRS, 0, layer, None)

            alone(0)
            loop(1, STAGES - 3, 0)
            for k in range(STAGES - 3, STAGES + 1):
                alone(k)
            loop(STAGES + 1, 2 * STAGES - 3, 1)
            for k in range(2 * STAGES - 3, 2 * STAGES):
                alone(k)

        def part_columns(part):
            return slice(E * part, E * (part + 1))

        def raw_weights(layer, part):
            return w_raw_kv[:, part - 1] if layer == 0 and part in (1, 2) else w_raw[:]

        @block.sync
        def _(sp):
            def rows_of(tensor, first_pair, pairs):
                return tensor.rearrange("(t p) e -> p t e", p=P)[:, bass.ds(first_pair, pairs), :]

            def load_weights(layer, part):
                wqkv, _, wproj, _ = weights[layer]
                src = wproj if part == 3 else wqkv[:, part_columns(part)]
                sp.dma_start(raw_weights(layer, part), src.rearrange("(kt p) c -> p kt c", p=P)).then_inc(w_loaded[part], 16)

            def load_bproj(layer):
                sp.dma_start(bias_out[:], weights[layer][3].partition_broadcast(P)).then_inc(bproj_loaded, 16)

            def store(pair, layer, q, par):
                sp.dma_start(rows_of(out if layer else hidden, pair - layer * LAYER_PAIRS, 1),
                             x_res[:, par, q:q + 1, :]).then_inc(stored[q], 16)

            for b in (2, 3):
                sp.sem_inc(stored[b], 16)
            sp.dma_start(x_in[:], rows_of(x, 0, PAIRS)).then_inc(x_loaded, 16)
            load_weights(0, 0)
            for layer in range(2):
                sp.dma_start(bias_qkv[:, layer, :], weights[layer][1]).then_inc(bias_loaded, 16)
            load_weights(0, 1)
            for half in range(2):
                sp.dma_start(adj_in[NODES * half:NODES * (half + 1), :], adj).then_inc(adj_loaded, 16)
            load_weights(0, 2)
            load_bproj(0)
            sp.wait_ge(w_lo_done, 1)
            load_weights(0, 3)
            sp.wait_ge(xT_ready, PAIRS)
            sp.wait_ge(x_res_done, PAIRS)
            sp.dma_start(x_in[:], rows_of(x, PAIRS, PAIRS)).then_inc(x_loaded, 16)
            sp.wait_ge(w_lo_done, PARTS)
            sp.wait_ge(bias_mixed, 1)
            load_weights(1, 0)

            def stage(n, par, layer, k):
                for p in range(PAIRS):
                    if (k, p) in LOADED:
                        part = LOADED[k, p]
                        sp.wait_ge(w_lo_done, PARTS + part)
                        load_weights(1, part)
                    q = (p + 2) % 4
                    if not (k == FIRST and p < 2):
                        sp.wait_ge(normed_done, n + p - 1).then_inc(store_begun, 1)
                        if k != FIRST:
                            sp.wait_ge(stored[q], 4 * n)
                        store(n + p - 2, 0 if k == REFRESH_PROJ and p < 2 else layer, q, par if p > 1 else 1 - par)
                    if p == 2 and k not in (LAST - 1, LAST):
                        sp.wait_ge(xT_ready, n + 2 * PAIRS)
                        sp.wait_ge(x_res_done, n + 2 * PAIRS)
                        if k in (REFRESH_QK, REFRESH_V):
                            for b in range(PAIRS):
                                sp.wait_ge(stored[b], 16 * 2 + 16 * (b // 2))
                            sp.dma_start(x_in[:], rows_of(hidden, n + 2 * PAIRS - LAYER_PAIRS, PAIRS)).then_inc(x_loaded, 16)
                        elif layer:
                            if k == REFRESH_PROJ:
                                for b in range(PAIRS):
                                    sp.wait_ge(stored[b], 16 * STAGES + 16 * (b // 2))
                            sp.dma_start(x_in[:], rows_of(hidden, n + 2 * PAIRS - LAYER_PAIRS, PAIRS)).then_inc(x_loaded, 16)
                        else:
                            sp.dma_start(x_in[:], rows_of(x, n + 2 * PAIRS, PAIRS)).then_inc(x_loaded, 16)
                    if (k, p) == (REFRESH_QK, 3):
                        sp.wait_ge(x_res_done, LAYER_PAIRS)
                        load_bproj(1)

            stages(sp, stage)
            for pair in (ALL_PAIRS - 2, ALL_PAIRS - 1):
                sp.wait_ge(normed_done, pair + 1)
                sp.wait_ge(stored[pair % 4], 4 * ALL_PAIRS)
                store(pair, 1, pair % 4, 1)
            for b in range(PAIRS):
                sp.wait_ge(stored[b], 2 * 16 * STAGES + 16 * (b // 2))

        @block.tensor
        def _(pe):
            def transpose_x(n, k):
                pe.wait_ge(x_loaded, 4 * n + 16)
                for ft in range(KT):
                    if k == BEFORE:
                        pass
                    elif ft < LANES:
                        pe.wait_ge(unit_saved[ft], n)
                    elif k == FIRST:
                        pe.wait_ge(bias_out_done, 1)
                    else:
                        pe.wait_ge(residual_done, n - PAIRS - 1)
                    for t in range(PAIRS):
                        last = nc.tensor.transpose(acc[:, ft, P * t:P * (t + 1)],
                                                   x_in[:, t, P * ft:P * (ft + 1)], ident[:])
                    last.then_inc(xT_ready, 1)

            def unit(u, n, fresh=None):
                lane, turn = unit_place(u)
                if fresh is not None and u % 4 == 0:
                    pe.wait_ge(w_lo_done, PARTS * fresh + u // 4 + 1)
                if turn == 0:
                    pe.wait_ge(xT_lo_done, n + PAIRS)
                else:
                    pe.wait_ge(unit_saved[lane], n + turn)
                for kt in range(KT):
                    for i, (w, xt) in enumerate(((w_hi, xT_hi), (w_hi, xT_lo), (w_lo, xT_hi))):
                        if u < 8:
                            fixed, moving = w[:, kt, P * u:P * (u + 1)], xt[:, kt, :]
                        else:
                            fixed, moving = xt[:, kt, P * (u - 8):P * (u - 7)], w[:, kt, V0:PROJ0]
                        last = nc.tensor.matmul(acc[:, lane, :], fixed, moving,
                                                start=(kt == 0 and i == 0), stop=(kt == KT - 1 and i == 2))
                last.then_inc(unit_ready[lane], 1)

            def scores(n, p):
                pe.wait_ge(operands_lo_done, n + p + 1)
                for blk in range(BLK):
                    cols = slice(256 * (blk % 2), 256 * (blk % 2 + 1))
                    for b in range(2):
                        for i, (q, k) in enumerate(((q_hi, k_hi), (q_hi, k_lo), (q_lo, k_hi))):
                            last = nc.tensor.matmul(att[:, blk // 2, cols], q[:, blk, b, :],
                                                    k[:, blk, b, :, :].rearrange("p a m -> p (a m)"),
                                                    start=(b == 0 and i == 0), stop=(b == 1 and i == 2))
                last.then_inc(scores_ready, 1)

            def transpose_probs(n, p):
                pe.wait_ge(probs_done, n + p)
                for t in range(8):
                    last = nc.tensor.transpose(att[:, 2 + t // 4, P * (t % 4):P * (t % 4 + 1)],
                                               probs[:, (p + 1) % 2, P * t:P * (t + 1)], ident[:])
                last.then_inc(probsT_ready, 1)

            def attend(n, p, par, drained):
                q = (p + 3) % 4
                vpar = par if p else 1 - par
                if drained:
                    pe.wait_ge(masked_done, n + p + 1)
                if p == 1:
                    for i in range(LANES):
                        pe.wait_ge(unit_saved[i], n + PAIRS)
                pe.wait_ge(probsT_saved, n + p).then_inc(attend_begun, 1)
                for a in range(4):
                    for j in range(2):
                        for s in range(2):
                            rows = slice(NODES * s, NODES * (s + 1))
                            for b in range(2):
                                last = nc.tensor.matmul(
                                    att[DH * a:DH * (a + 1), s, P * j + NODES * b:P * j + NODES * (b + 1)],
                                    v_sel[rows, vpar, q, b, P * j + DH * a:P * j + DH * (a + 1)],
                                    probsT[rows, P * (2 * a + j) + NODES * b:P * (2 * a + j) + NODES * (b + 1)],
                                    start=True, stop=True)
                last.then_inc(yT_ready, 1)

            def project(n, p, k):
                if (k, p) == (FIRST, 1):
                    pe.wait_ge(w_lo_done, PARTS)
                if (k, p) == (REFRESH_PROJ, 1):
                    pe.wait_ge(w_lo_done, 2 * PARTS)
                pe.wait_ge(yT_lo_done, n + p)
                if not (k == FIRST and p == 1):
                    pe.wait_ge(residual_done, n + p - 1)
                for blk in range(BLK):
                    for i, (w, yt) in enumerate(((w_hi, yT_hi), (w_lo, yT_hi), (w_hi, yT_lo))):
                        last = nc.tensor.matmul(acc[:, 3, :], yt[:, blk % 2, P * (blk // 2):P * (blk // 2 + 1)],
                                                w[:, blk, PROJ0:WCOLS],
                                                start=(blk == 0 and i == 0), stop=(blk == BLK - 1 and i == 2))
                last.then_inc(proj_ready, 1)

            def mix_bias(layer, bank):
                pe.wait_ge(wide_done, layer + 1)
                pe.wait_ge(w_loaded[3], 16 * (layer + 1))
                for kt in range(KT):
                    last = nc.tensor.matmul(bank, bias_v_wide[:, kt, :], w_raw[:, kt, :],
                                            start=(kt == 0), stop=(kt == KT - 1))
                last.then_inc(bias_mixed, 1)

            pe.wait_ge(consts_done, 5)
            transpose_x(0, BEFORE)
            for u in range(UNITS):
                unit(u, 0, fresh=0)
                if u == 7:
                    mix_bias(0, acc[:, 3, :])

            def stage(n, par, layer, k):
                fresh = 1 if k == REFRESH_V else None
                if k != LAST:
                    transpose_x(n + PAIRS, k)
                for p in range(PAIRS):
                    before = not (k == FIRST and p == 0)
                    scores(n, p)
                    if k != LAST:
                        unit(3 * p, n + PAIRS, fresh)
                    if before:
                        if (k, p) == (REFRESH_V, 2):
                            pe.wait_ge(bias_out_done, 2)
                        transpose_probs(n, p)
                    if k != LAST:
                        unit(3 * p + 1, n + PAIRS, fresh)
                    if before:
                        attend(n, p, par, True)
                    if (k, p) == (REFRESH_V, 1):
                        mix_bias(1, att[:, 2, :])
                    if k != LAST:
                        unit(3 * p + 2, n + PAIRS, fresh)
                    if before:
                        project(n, p, k)

            stages(pe, stage)
            transpose_probs(ALL_PAIRS, 0)
            attend(ALL_PAIRS, 0, 0, False)
            project(ALL_PAIRS, 0, None)

        @block.scalar
        def _(act):
            def split_x(n):
                for ft in range(KT):
                    act.wait_ge(xT_ready, n + ft + 1)
                    nc.scalar.activation(xT_hi[:, ft, :], acc[:, ft, :], ACT.Copy).then_inc(xT_hi_done, 1)

            def save(u, n, par, layer):
                lane, turn = unit_place(u)
                act.wait_ge(unit_ready[lane], n + turn + 1)
                if u < 8:
                    nc.scalar.activation(qkT[:, par, u, :], acc[:, lane, :], ACT.Identity,
                                         bias=bias_qkv[:, layer, u:u + 1]).then_inc(unit_saved[lane], 1)
                    return
                for b in range(2):
                    for s in range(2):
                        src = acc[NODES * b:NODES * (b + 1), lane, :].rearrange("t (j s c) -> t s j c", j=2, s=2)
                        dst = v_sel[NODES * s:NODES * (s + 1), par, u - 8, b, :].rearrange("t (j c) -> t j c", j=2)
                        last = nc.scalar.activation(dst, src[:, s, :, :], ACT.Copy)
                last.then_inc(unit_saved[lane], 1)

            def operands_hi(n, p, par, free):
                if p == 0:
                    act.wait_ge(unit_saved[0], n + 3)
                    act.wait_ge(unit_saved[1], n + 3)
                    act.wait_ge(unit_saved[2], n + 2)
                if free:
                    act.wait_ge(scores_ready, n + p)
                for dst, src in operand_places(q_hi, k_hi, par, p):
                    last = nc.scalar.activation(dst, src, ACT.Copy)
                last.then_inc(operands_hi_done, 1)

            def save_probsT(n, p):
                act.wait_ge(probsT_ready, n + p)
                nc.scalar.activation(probsT[:].rearrange("t (b c) -> t b c", b=2), att[:, 2:4, :],
                                     ACT.Copy).then_inc(probsT_saved, 1)

            def split_y(n, p):
                act.wait_ge(yT_ready, n + p)
                nc.scalar.activation(yT_hi[:], att[:, 0:2, 0:2 * P], ACT.Copy).then_inc(yT_hi_done, 1)

            def split_weights(layer, part):
                act.wait_ge(w_loaded[part], 16 * (layer + 1))
                nc.scalar.activation(w_hi[:, :, part_columns(part)], raw_weights(layer, part), ACT.Copy).then_inc(w_hi_done, 1)

            split_x(0)
            split_weights(0, 0)
            split_weights(0, 1)
            act.wait_ge(bias_loaded, 32)
            for u in range(UNITS):
                save(u, 0, 0, 0)
                if u == 0:
                    split_weights(0, 2)
                if u == 2:
                    split_weights(0, 3)
                if u == 7:
                    act.wait_ge(operands_zeroed, 4)
                    operands_hi(0, 0, 0, False)

            def stage(n, par, layer, k):
                product_layer = 1 if k == REFRESH_V else layer
                if k != LAST:
                    split_x(n + PAIRS)
                for p in range(PAIRS):
                    before = not (k == FIRST and p == 0)
                    if (k, p) == (REFRESH_PROJ, 1):
                        act.wait_ge(proj_ready, LAYER_PAIRS)
                        split_weights(1, 3)
                    if p < 3:
                        operands_hi(n, p + 1, par, True)
                    elif k != LAST:
                        operands_hi(n + PAIRS, 0, 1 - par, True)
                    if k != LAST:
                        save(3 * p, n + PAIRS, 1 - par, product_layer)
                    if before:
                        save_probsT(n, p)
                    act.wait_ge(shifted_done, n + p + 1)
                    nc.scalar.activation(probs[:, p % 2, :], probs[:, p % 2, :], ACT.Exp,
                                         scale=SCALE).then_inc(exp_done, 1)
                    if k != LAST:
                        save(3 * p + 1, n + PAIRS, 1 - par, product_layer)
                    if before:
                        split_y(n, p)
                    if (k, p) in REFRESHED:
                        split_weights(1, REFRESHED[k, p])
                    if k != LAST:
                        save(3 * p + 2, n + PAIRS, 1 - par, product_layer)

            stages(act, stage)
            save_probsT(ALL_PAIRS, 0)
            split_y(ALL_PAIRS, 0)

        @block.vector
        def _(dve):
            def by_head(ap):
                return ap.unsqueeze(2).broadcast_to([P, HEADS, NODES])

            def split_x(n):
                for ft in range(KT):
                    dve.wait_ge(xT_hi_done, n + ft + 1)
                    nc.vector.tensor_tensor(xT_lo[:, ft, :], acc[:, ft, :], xT_hi[:, ft, :].bitcast(F32),
                                            ALU.subtract).then_inc(xT_lo_done, 1)

            def shift_scores(n, p):
                heads = probs[:, p % 2, :].rearrange("t (h m) -> t h m", h=HEADS)
                dve.wait_ge(scores_ready, n + p + 1)
                nc.vector.tensor_tensor(
                    probs[:, p % 2, :].rearrange("t (a b m) -> t b a m", a=4, b=BLK),
                    att[:, 0:2, :].rearrange("t g (b a m) -> t (g b) a m", a=4, b=2),
                    mask[:].unsqueeze(1).unsqueeze(1).broadcast_to([P, BLK, 4, NODES]),
                    ALU.add).then_inc(masked_done, 1)
                dve.wait_ge(masked_done, n + p + 1)
                nc.vector.tensor_reduce(row_max[:], heads, AX_X, ALU.max).then_inc(max_done, 1)
                dve.wait_ge(max_done, n + p + 1)
                nc.vector.tensor_tensor(heads, heads, by_head(row_max[:]), ALU.subtract).then_inc(shifted_done, 1)

            def operands_lo(n, p, par):
                dve.wait_ge(operands_hi_done, n + p + 1)
                for (dst, src), (hi, _) in zip(operand_places(q_lo, k_lo, par, p), operand_places(q_hi, k_hi, par, p)):
                    last = nc.vector.tensor_tensor(dst, src, hi.bitcast(F32), ALU.subtract)
                last.then_inc(operands_lo_done, 1)

            def sum_probs(n, p):
                heads = probs[:, p % 2, :].rearrange("t (h m) -> t h m", h=HEADS)
                dve.wait_ge(exp_done, n + p + 1)
                nc.vector.tensor_reduce(row_sum[:], heads, AX_X, ALU.add).then_inc(sum_done, 1)
                dve.wait_ge(sum_done, n + p + 1)
                nc.vector.reciprocal(row_inv[:], row_sum[:]).then_inc(inv_done, 1)

            def normalise_probs(n, p):
                heads = probs[:, p % 2, :].rearrange("t (h m) -> t h m", h=HEADS)
                dve.wait_ge(inv_done, n + p + 1)
                nc.vector.tensor_tensor(heads, heads, by_head(row_inv[:]), ALU.mult).then_inc(probs_done, 1)

            def split_y(n, p):
                dve.wait_ge(yT_hi_done, n + p)
                nc.vector.tensor_tensor(yT_lo[:], att[:, 0:2, 0:2 * P], yT_hi[:].bitcast(F32),
                                        ALU.subtract).then_inc(yT_lo_done, 1)

            def residual(n, p, par):
                q = (p + 3) % 4
                rpar = par if p else 1 - par
                dve.wait_ge(proj_ready, n + p)
                dve.wait_ge(x_res_done, n + p)
                nc.vector.tensor_tensor(x_res[:, rpar, q, :], acc[:, 3, :], x_res[:, rpar, q, :],
                                        ALU.add).then_inc(residual_done, 1)
                dve.wait_ge(residual_done, n + p)
                nc.vector.bn_stats(stats[:], x_res[:, rpar, q, :]).then_inc(stats_done, 1)
                dve.wait_ge(stats_done, n + p).then_inc(aggregate_begun, 1)
                nc.vector.bn_aggr(mean_var[:, q % 2, :], stats[:]).then_inc(mean_var_done, 1)

            def normalise(n, p, par):
                q = (p + 2) % 4
                rpar = par if p > 1 else 1 - par
                dve.wait_ge(rstd_done, n + p - 1)
                nc.vector.tensor_scalar(x_res[:, rpar, q, :], x_res[:, rpar, q, :], mean_var[:, q % 2, 0:1],
                                        rstd[:, q % 2:q % 2 + 1], ALU.subtract, ALU.mult).then_inc(normed_done, 1)

            def split_weights(layer, part):
                dve.wait_ge(w_hi_done, PARTS * layer + part + 1)
                cols = part_columns(part)
                nc.vector.tensor_tensor(w_lo[:, :, cols], raw_weights(layer, part), w_hi[:, :, cols].bitcast(F32),
                                        ALU.subtract).then_inc(w_lo_done, 1)

            def widen_bias(layer):
                nc.vector.tensor_copy(bias_v_wide[:], bias_qkv[:, layer, 8:12].unsqueeze(2)
                                      .broadcast_to([P, KT, P])).then_inc(wide_done, 1)

            def finish_bias(layer, bank):
                dve.wait_ge(bproj_loaded, 16 * (layer + 1))
                dve.wait_ge(bias_mixed, layer + 1)
                nc.vector.tensor_tensor(bias_out[:], bank, bias_out[:], ALU.add).then_inc(bias_out_done, 1)

            split_x(0)
            split_weights(0, 0)
            split_weights(0, 1)
            dve.wait_ge(adj_loaded, 32)
            dve.wait_ge(consts_done, 5)
            nc.vector.tensor_tensor(mask[:], adj_in[:], eye[:], ALU.add).then_inc(setup, 1)
            dve.wait_ge(setup, 1)
            nc.vector.tensor_scalar(mask[:], mask[:], 0.0, 1.0, ALU.is_gt, ALU.subtract).then_inc(setup, 1)
            dve.wait_ge(setup, 2)
            nc.vector.tensor_scalar(mask[:], mask[:], -MASKED, None, ALU.mult).then_inc(setup, 1)
            dve.wait_ge(setup, 3)
            dve.wait_ge(bias_loaded, 32)
            widen_bias(0)
            split_weights(0, 2)
            split_weights(0, 3)
            dve.wait_ge(operands_zeroed, 4)
            operands_lo(0, 0, 0)
            finish_bias(0, acc[:, 3, :])
            widen_bias(1)

            def stage(n, par, layer, k):
                if k != LAST:
                    split_x(n + PAIRS)
                for p in range(PAIRS):
                    shift_scores(n, p)
                    if (k, p) == (REFRESH_PROJ, 1):
                        split_weights(1, 3)
                    if not (k == FIRST and p < 2):
                        normalise(n, p, par)
                    if p < 3:
                        operands_lo(n, p + 1, par)
                    elif k != LAST:
                        operands_lo(n + PAIRS, 0, 1 - par)
                    sum_probs(n, p)
                    if not (k == FIRST and p == 0):
                        split_y(n, p)
                    normalise_probs(n, p)
                    if (k, p) in REFRESHED:
                        split_weights(1, REFRESHED[k, p])
                    if (k, p) == (REFRESH_V, 1):
                        finish_bias(1, att[:, 2, :])
                    if not (k == FIRST and p == 0):
                        residual(n, p, par)

            stages(dve, stage)
            normalise(ALL_PAIRS, 0, 0)
            split_y(ALL_PAIRS, 0)
            residual(ALL_PAIRS, 0, 0)
            normalise(ALL_PAIRS, 1, 0)

        @block.gpsimd
        def _(pool):
            nc.gpsimd.memset(ident[:], 0.0).then_inc(zeroed, 1)
            nc.gpsimd.memset(eye[:], 0.0).then_inc(zeroed, 1)
            for t in (q_hi, q_lo, k_hi, k_lo):
                nc.gpsimd.memset(t[:].bitcast(F32), 0.0).then_inc(operands_zeroed, 1)
            nc.gpsimd.memset(minus_half[:], -0.5).then_inc(consts_done, 1)
            nc.gpsimd.memset(epsilon[:], EPS).then_inc(consts_done, 1)
            pool.wait_ge(zeroed, 2)
            nc.gpsimd.affine_select(out=ident[:], in_=ident[:], compare_op=ALU.not_equal, fill=1.0, base=0,
                                    pattern=[[-1, P]], channel_multiplier=1).then_inc(consts_done, 1)
            nc.gpsimd.affine_select(out=eye[:], in_=eye[:], compare_op=ALU.not_equal, fill=1.0, base=0,
                                    pattern=[[-1, NODES]], channel_multiplier=1).then_inc(consts_done, 1)
            pool.wait_ge(consts_done, 4)
            nc.gpsimd.affine_select(out=eye[:], in_=eye[:], compare_op=ALU.not_equal, fill=1.0, base=-NODES,
                                    pattern=[[-1, NODES]], channel_multiplier=1).then_inc(consts_done, 1)

            def add_bias(n, par, k):
                pool.wait_ge(x_loaded, 4 * n + 16)
                for t in range(PAIRS):
                    if k != FIRST:
                        pool.wait_ge(stored[t], 4 * n - 16 + 16 * (t // 2))
                    nc.gpsimd.tensor_tensor(x_res[:, par, t, :], x_in[:, t, :], bias_out[:], ALU.add).then_inc(x_res_done, 1)

            def inverse_deviation(n, p):
                q = (p + 3) % 2
                pool.wait_ge(mean_var_done, n + p)
                nc.gpsimd.tensor_tensor(var_eps[:], mean_var[:, q, 1:2], epsilon[:], ALU.add).then_inc(var_eps_done, 1)
                pool.wait_ge(var_eps_done, n + p)
                nc.gpsimd.tensor_tensor(rstd[:, q:q + 1], var_eps[:], minus_half[:], ALU.pow).then_inc(rstd_done, 1)

            pool.wait_ge(bias_out_done, 1)
            add_bias(0, 0, FIRST)

            def stage(n, par, layer, k):
                for p in range(PAIRS):
                    if p == 2 and k != LAST:
                        if k == REFRESH_V:
                            pool.wait_ge(bias_out_done, 2)
                        add_bias(n + PAIRS, 1 - par, k)
                    if not (k == FIRST and p == 0):
                        inverse_deviation(n, p)

            stages(pool, stage)
            inverse_deviation(ALL_PAIRS, 0)


_WEIGHTS = ["Wqkv", "bqkv", "Wproj", "bproj"]


def kernel(**inputs):
    import numpy as _np
    import concourse.bacc as _bacc
    from concourse import mybir as _mybir
    from concourse.bass_utils import run_bass_kernel_spmd as _run

    nc = _bacc.Bacc("TRN2", target_bir_lowering=False, num_devices=1)
    arrays = {}

    def given(name, shape=None):
        a = _np.asarray(inputs[name])
        a = a.reshape(shape) if shape else a
        if name.endswith("bqkv"):
            a = a.reshape(-1, P).T
        a = _np.ascontiguousarray(a)
        arrays[f"in_{name}"] = a
        return nc.dram_tensor(f"in_{name}", a.shape, _mybir.dt.from_np(a.dtype), kind="ExternalInput").ap()

    x = given("x", (TOKENS, E))
    adj = given("adj")
    weights = [[given(f"L{layer}_gnn_{w}") for w in _WEIGHTS] for layer in range(2)]
    out = nc.dram_tensor("out", (TOKENS, E), F32, kind="ExternalOutput").ap()
    build(nc, x, adj, weights, out)
    r = _run(nc, [arrays], core_ids=[0])
    return _np.asarray(r.results[0]["out"]).reshape(inputs["x"].shape)
```

```python
from contextlib import ExitStack

import concourse.bass as bass
import concourse.mybir as mybir

F32 = mybir.dt.float32
F32R = mybir.dt.float32r
I32 = mybir.dt.int32
ALU = mybir.AluOpType
ACT = mybir.ActivationFunctionType
AX_X = mybir.AxisListType.X

P = 128
NODES = 64
E = 512
HEADS = 16
DH = E // HEADS
TOKENS = 128 * NODES
GROUP = 512
STAGES = TOKENS // GROUP
PAIRS = GROUP // P
KT = E // P
SQ = 32
BLK = 4
WCOLS = 4 * E
V0, PROJ0 = 2 * E, 3 * E
PARTS = WCOLS // E
LAYER_PAIRS = STAGES * PAIRS
ALL_PAIRS = 2 * LAYER_PAIRS
FIRST, REFRESH_QK, REFRESH_V, REFRESH_PROJ, LAST = 0, STAGES - 2, STAGES - 1, STAGES, 2 * STAGES - 1
REFRESHED = {(REFRESH_QK, 2): 0, (REFRESH_QK, 3): 1, (REFRESH_V, 0): 2}
LOADED = {(REFRESH_QK, 3): 1, (REFRESH_V, 0): 2, (REFRESH_V, 1): 3}
EPS = 1e-5
MASKED = -3.0e38
SCALE = float(DH) ** -0.5
UNITS = 12
LANES = 3


def build(nc, x, adj, weights, out):
    ctx = ExitStack()
    with ctx:
        def sb(name, shape, dt=F32):
            return ctx.enter_context(nc.sbuf_tensor(name, shape, dt))

        def sem(name):
            return ctx.enter_context(nc.semaphore(name))

        hidden = nc.dram_tensor("hidden", [TOKENS, E], F32).ap()

        w_hi = sb("w_hi", [P, KT, WCOLS], F32R)
        w_lo = sb("w_lo", [P, KT, WCOLS], F32R)
        w_raw = sb("w_raw", [P, KT, E])
        bias_qkv = sb("bias_qkv", [P, 2, 12])
        bias_out = sb("bias_out", [P, 2, E])
        x_in = sb("x_in", [P, GROUP // SQ, P])
        x_res = sb("x_res", [P, PAIRS, E])
        xT = sb("xT", [P, KT, GROUP])
        bias_v_wide = xT[:, 0, :].rearrange("p (kt m) -> p kt m", kt=KT)
        xT_hi = sb("xT_hi", [P, KT, GROUP], F32R)
        xT_lo = sb("xT_lo", [P, KT, GROUP], F32R)
        qkT = sb("qkT", [P, 2, 8, GROUP])
        w_raw_kv = qkT[:, 1].rearrange("p (i kt) t -> p i kt t", i=2)
        k_diag = sb("k_diag", [P, BLK, 2, 4, NODES])
        v_diag = sb("v_diag", [P, 2, PAIRS, 2, HEADS // 2, 2 * DH])
        probs = sb("probs", [P, 2, HEADS * NODES])
        probsT = sb("probsT", [P, 2 * GROUP])
        yT_hi = sb("yT_hi", [P, KT, P], F32R)
        yT_lo = sb("yT_lo", [P, KT, P], F32R)
        row_max = sb("row_max", [P, HEADS])
        row_sum = sb("row_sum", [P, HEADS])
        row_inv = sb("row_inv", [P, HEADS])
        stats = sb("stats", [P, 6])
        mean_var = sb("mean_var", [P, 2, 2])
        var_eps = sb("var_eps", [P, 1])
        rstd = sb("rstd", [P, 2])
        minus_half = sb("minus_half", [P, 1])
        epsilon = sb("epsilon", [P, 1])
        ident = sb("ident", [P, P])
        eye = sb("eye", [P, NODES])
        adj_in = sb("adj_in", [P, NODES], I32)
        mask = sb("mask", [P, NODES])
        acc = ctx.enter_context(nc.psum_tensor("acc", [P, 4, 512], F32))
        att = ctx.enter_context(nc.psum_tensor("att", [P, 4, 512], F32))

        adj_loaded = sem("adj_loaded")
        x_in_loaded = sem("x_in_loaded")
        x_res_loaded = [sem(f"x_res_loaded{b}") for b in range(PAIRS)]
        w_loaded = [sem(f"w_loaded{part}") for part in range(PARTS)]
        bias_loaded = sem("bias_loaded")
        stored = [sem(f"stored{b}") for b in range(PAIRS)]
        load_begun = sem("load_begun")
        bias_mixed = sem("bias_mixed")
        unit_ready = [sem(f"unit_ready{i}") for i in range(LANES)]
        scores_ready = sem("scores_ready")
        probsT_ready = sem("probsT_ready")
        yT_ready = sem("yT_ready")
        proj_ready = sem("proj_ready")
        attend_begun = sem("attend_begun")
        w_hi_done = sem("w_hi_done")
        xT_hi_done = sem("xT_hi_done")
        unit_saved = [sem(f"unit_saved{i}") for i in range(LANES)]
        exp_done = sem("exp_done")
        probsT_saved = sem("probsT_saved")
        yT_hi_done = sem("yT_hi_done")
        k_placed = sem("k_placed")
        setup = sem("setup")
        wide_done = sem("wide_done")
        xT_ready = sem("xT_ready")
        w_lo_done = sem("w_lo_done")
        bias_out_done = sem("bias_out_done")
        xT_lo_done = sem("xT_lo_done")
        masked_done = sem("masked_done")
        max_done = sem("max_done")
        shifted_done = sem("shifted_done")
        sum_done = sem("sum_done")
        inv_done = sem("inv_done")
        probs_done = sem("probs_done")
        yT_lo_done = sem("yT_lo_done")
        residual_done = sem("residual_done")
        stats_done = sem("stats_done")
        mean_var_done = sem("mean_var_done")
        aggregate_begun = sem("aggregate_begun")
        normed_done = sem("normed_done")
        zeroed = sem("zeroed")
        k_zeroed = sem("k_zeroed")
        v_zeroed = sem("v_zeroed")
        consts_done = sem("consts_done")
        x_res_done = sem("x_res_done")
        var_eps_done = sem("var_eps_done")
        rstd_done = sem("rstd_done")

        block = ctx.enter_context(nc.Block())

        def unit_place(u):
            return u % LANES, u // LANES

        def slot_units(k, p):
            if k == LAST - 1 and p >= 2:
                return (6, 7, None) if p == 2 else (None, None, 8)
            if k == LAST:
                return None, None, 9 + p if p < 3 else None
            return 3 * p, 3 * p + 1, 3 * p + 2

        def units_group(n, par, k):
            return (n, par) if k == LAST else (n + PAIRS, 1 - par)

        def tail(k, p):
            return k == LAST or (k, p) == (LAST - 1, 3)

        def stages(eng, stage):
            def alone(k):
                stage(PAIRS * k, k % 2, int(k >= STAGES), k)

            def loop(k, end, layer):
                with eng.Fori(PAIRS * k, PAIRS * (end - 2) + 1, 2 * PAIRS) as n:
                    stage(n, 1, layer, None)
                    stage(n + PAIRS, 0, layer, None)

            alone(0)
            loop(1, STAGES - 3, 0)
            for k in range(STAGES - 3, STAGES + 1):
                alone(k)
            loop(STAGES + 1, 2 * STAGES - 3, 1)
            for k in range(2 * STAGES - 3, 2 * STAGES):
                alone(k)

        def part_columns(part):
            return slice(E * part, E * (part + 1))

        def raw_weights(layer, part):
            return w_raw_kv[:, part - 1] if layer == 0 and part in (1, 2) else w_raw[:]

        @block.sync
        def _(sp):
            def rows(layer, pair):
                return (hidden if layer else x).rearrange("(t p) e -> p t e", p=P)[:, bass.ds(pair - layer * LAYER_PAIRS, 1), :]

            def load_x_res(layer, pair, q):
                sp.dma_start(x_res[:, q:q + 1, :], rows(layer, pair)).then_inc(x_res_loaded[q], 16)

            def load_x_in(layer, n):
                group = (hidden if layer else x).rearrange("(t b r) (i f) -> i r t b f", b=P // SQ, r=SQ, i=4)
                for i in range(4):
                    src = group[i][:, bass.ds(n - layer * LAYER_PAIRS, PAIRS)].rearrange("r t b f -> r (t b) f")
                    sp.dma_start(x_in[SQ * i:SQ * (i + 1)], src).then_inc(x_in_loaded, 16)

            def load_weights(layer, part):
                wqkv, _, wproj, _ = weights[layer]
                dst = raw_weights(layer, part)
                if part == 3:
                    sp.dma_start(dst, wproj.rearrange("(kt p) c -> p kt c", p=P)).then_inc(w_loaded[part], 16)
                    return
                src = wqkv[:, part_columns(part)].rearrange("(i f c) n -> i c f n", i=4, c=SQ)
                for i in range(4):
                    sp.dma_start(dst[SQ * i:SQ * (i + 1)], src[i]).then_inc(w_loaded[part], 16)

            def store(layer, pair, q):
                dst = (out if layer else hidden).rearrange("(t p) e -> p t e", p=P)
                sp.dma_start(dst[:, bass.ds(pair - layer * LAYER_PAIRS, 1), :], x_res[:, q:q + 1, :]).then_inc(stored[q], 16)

            load_x_in(0, 0)
            load_weights(0, 0)
            for layer in range(2):
                sp.dma_start(bias_qkv[:, layer, :], weights[layer][1]).then_inc(bias_loaded, 16)
            load_weights(0, 1)
            sp.wait_ge(xT_ready, PAIRS)
            load_x_in(0, PAIRS)
            for half in range(2):
                sp.dma_start(adj_in[NODES * half:NODES * (half + 1), :], adj).then_inc(adj_loaded, 16)
            load_weights(0, 2)
            for layer in range(2):
                sp.dma_start(bias_out[:, layer, :], weights[layer][3].partition_broadcast(P)).then_inc(bias_loaded, 16)
            sp.wait_ge(w_lo_done, 1)
            load_weights(0, 3)
            for q in range(PAIRS):
                load_x_res(0, q, q)
            sp.wait_ge(w_lo_done, PARTS)
            sp.wait_ge(bias_mixed, 1)
            load_weights(1, 0)

            def stage(n, par, layer, k):
                for p in range(PAIRS):
                    if (k, p) in LOADED:
                        part = LOADED[k, p]
                        sp.wait_ge(w_lo_done, PARTS + part)
                        load_weights(1, part)
                    if p == 0 and k not in (LAST - 1, LAST):
                        if k == REFRESH_QK:
                            for b in range(PAIRS):
                                sp.wait_ge(stored[b], 16 * 3)
                        sp.wait_ge(xT_ready, n + 2 * PAIRS)
                        load_x_in(1 if k in (REFRESH_QK, REFRESH_V) else layer, n + 2 * PAIRS)
                    if (k, p) == (REFRESH_PROJ, 3):
                        for b in range(PAIRS):
                            sp.wait_ge(stored[b], 16 * STAGES)
                    if not (k == FIRST and p < 3) and not (k == LAST and p == 3):
                        sp.wait_ge(stored[(p + 1) % 4], 4 * n + 16 * (p // 3)).then_inc(load_begun, 1)
                        load_x_res(1 if (k, p) == (REFRESH_V, 3) else layer, n + p + 1, (p + 1) % 4)
                    if not (k == FIRST and p < 2):
                        sp.wait_ge(normed_done, n + p - 1)
                        store(0 if k == REFRESH_PROJ and p < 2 else layer, n + p - 2, (p + 2) % 4)

            stages(sp, stage)
            for pair in (ALL_PAIRS - 2, ALL_PAIRS - 1):
                sp.wait_ge(normed_done, pair + 1)
                store(1, pair, pair % 4)
            for b in range(PAIRS):
                sp.wait_ge(stored[b], 2 * 16 * STAGES)

        @block.tensor
        def _(pe):
            def unit(u, n, fresh=None):
                lane, turn = unit_place(u)
                if fresh is not None and u % 4 == 0:
                    pe.wait_ge(w_lo_done, PARTS * fresh + u // 4 + 1)
                if not (fresh == 0 and turn == 0):
                    pe.wait_ge(unit_saved[lane], n + turn)
                for kt in range(KT):
                    if u == 0:
                        pe.wait_ge(xT_lo_done, n + kt + 1)
                    for i, (w, xt) in enumerate(((w_hi, xT_hi), (w_hi, xT_lo), (w_lo, xT_hi))):
                        if u < 8:
                            fixed, moving = w[:, kt, P * u:P * (u + 1)], xt[:, kt, :]
                        else:
                            fixed, moving = xt[:, kt, P * (u - 8):P * (u - 7)], w[:, kt, V0:PROJ0]
                        last = nc.tensor.matmul(acc[:, lane, :], fixed, moving,
                                                start=(kt == 0 and i == 0), stop=(kt == KT - 1 and i == 2))
                last.then_inc(unit_ready[lane], 1)

            def scores(n, p, par, k):
                if (k, p) == (FIRST, 1):
                    pe.wait_ge(masked_done, 1)
                pe.wait_ge(k_placed, n + p + 1)
                for blk in range(BLK):
                    for b in range(2):
                        last = nc.tensor.matmul(att[NODES * b:NODES * (b + 1), blk // 2, 256 * (blk % 2):256 * (blk % 2 + 1)],
                                                qkT[:, par, blk, P * p + NODES * b:P * p + NODES * (b + 1)],
                                                k_diag[:, blk, b, :, :].rearrange("p a m -> p (a m)"),
                                                start=True, stop=True)
                last.then_inc(scores_ready, 1)

            def transpose_probs(n, p):
                pe.wait_ge(probs_done, n + p)
                for t in range(8):
                    last = nc.tensor.transpose(att[:, 2 + t // 4, P * (t % 4):P * (t % 4 + 1)],
                                               probs[:, (p + 1) % 2, P * t:P * (t + 1)], ident[:])
                last.then_inc(probsT_ready, 1)

            def attend(n, p, par, drained, k):
                q = (p + 3) % 4
                vpar = par if p else 1 - par
                if drained:
                    pe.wait_ge(masked_done, n + p + 1)
                if k == LAST and p > 0:
                    lane, turn = unit_place(8 + p - 1)
                    pe.wait_ge(unit_saved[lane], n + turn + 1)
                elif p == 1:
                    for i in range(LANES):
                        pe.wait_ge(unit_saved[i], n + PAIRS)
                pe.wait_ge(probsT_saved, n + p).then_inc(attend_begun, 1)
                for t in range(KT):
                    for b in range(2):
                        for half in range(2):
                            heads = 2 * t + half
                            last = nc.tensor.matmul(
                                att[NODES * half:NODES * (half + 1), 0, P * t + NODES * b:P * t + NODES * (b + 1)],
                                v_diag[:, vpar, q, b, heads, :],
                                probsT[:, P * heads + NODES * b:P * heads + NODES * (b + 1)],
                                start=True, stop=True)
                last.then_inc(yT_ready, 1)

            def project(n, p, k):
                if (k, p) == (FIRST, 1):
                    pe.wait_ge(w_lo_done, PARTS)
                if (k, p) == (REFRESH_PROJ, 1):
                    pe.wait_ge(w_lo_done, 2 * PARTS)
                pe.wait_ge(yT_lo_done, n + p)
                if (k, p) == (FIRST, 1):
                    pe.wait_ge(bias_out_done, 1)
                else:
                    pe.wait_ge(residual_done, n + p - 1)
                for blk in range(BLK):
                    for i, (w, yt) in enumerate(((w_hi, yT_hi), (w_lo, yT_hi), (w_hi, yT_lo))):
                        last = nc.tensor.matmul(acc[:, 3, :], yt[:, blk, :],
                                                w[:, blk, PROJ0:WCOLS],
                                                start=(blk == 0 and i == 0), stop=(blk == BLK - 1 and i == 2))
                last.then_inc(proj_ready, 1)

            def mix_bias(layer, bank):
                pe.wait_ge(wide_done, layer + 1)
                pe.wait_ge(w_loaded[3], 16 * (layer + 1))
                for kt in range(KT):
                    last = nc.tensor.matmul(bank, bias_v_wide[:, kt, :], w_raw[:, kt, :],
                                            start=(kt == 0), stop=(kt == KT - 1))
                last.then_inc(bias_mixed, 1)

            pe.wait_ge(consts_done, 5)
            for u in range(UNITS):
                unit(u, 0, fresh=0)
                if u == 7:
                    mix_bias(0, acc[:, 3, :])

            def stage(n, par, layer, k):
                fresh = 1 if k == REFRESH_V else None
                group, _ = units_group(n, par, k)
                for p in range(PAIRS):
                    before = not (k == FIRST and p == 0)
                    units = slot_units(k, p)
                    scores(n, p, par, k)
                    if units[0] is not None:
                        unit(units[0], group, fresh)
                    if before:
                        if (k, p) == (REFRESH_V, 2):
                            pe.wait_ge(bias_out_done, 2)
                        transpose_probs(n, p)
                    if units[1] is not None:
                        unit(units[1], group, fresh)
                    if before:
                        attend(n, p, par, True, k)
                    if (k, p) == (REFRESH_V, 1):
                        mix_bias(1, att[:, 2, :])
                    if units[2] is not None:
                        unit(units[2], group, fresh)
                    if before:
                        project(n, p, k)

            stages(pe, stage)
            transpose_probs(ALL_PAIRS, 0)
            pe.wait_ge(unit_saved[unit_place(UNITS - 1)[0]], ALL_PAIRS)
            attend(ALL_PAIRS, 0, 0, False, None)
            project(ALL_PAIRS, 0, None)

        @block.scalar
        def _(act):
            def split_x(n, first=False):
                if not first:
                    act.wait_ge(unit_ready[2], n)
                for ft in range(KT):
                    act.wait_ge(xT_ready, n + ft + 1)
                    nc.scalar.activation(xT_hi[:, ft, :], xT[:, ft, :], ACT.Copy).then_inc(xT_hi_done, 1)

            def save(u, n, par, layer):
                lane, turn = unit_place(u)
                act.wait_ge(unit_ready[lane], n + turn + 1)
                if u < 8:
                    nc.scalar.activation(qkT[:, par, u, :], acc[:, lane, :], ACT.Identity,
                                         bias=bias_qkv[:, layer, u:u + 1]).then_inc(unit_saved[lane], 1)
                    return
                for b in range(2):
                    for half in range(2):
                        src = acc[NODES * b:NODES * (b + 1), lane, :].rearrange("t (h s c) -> t s h c", s=2, c=DH)
                        dst = v_diag[NODES * half:NODES * (half + 1), par, u - 8, b, :, DH * half:DH * (half + 1)]
                        last = nc.scalar.activation(dst, src[:, half, :, :], ACT.Copy)
                last.then_inc(unit_saved[lane], 1)

            def place_k(n, p, par, free):
                if p == 0:
                    act.wait_ge(unit_saved[0], n + 3)
                    act.wait_ge(unit_saved[1], n + 3)
                    act.wait_ge(unit_saved[2], n + 2)
                if free:
                    act.wait_ge(scores_ready, n + p)
                for a in range(4):
                    rows = slice(DH * a, DH * (a + 1))
                    src = qkT[rows, par, BLK:2 * BLK, P * p:P * (p + 1)].rearrange("p c (b t) -> p c b t", b=2)
                    last = nc.scalar.activation(k_diag[rows, :, :, a, :], src, ACT.Copy)
                last.then_inc(k_placed, 1)

            def save_probsT(n, p):
                act.wait_ge(probsT_ready, n + p)
                nc.scalar.activation(probsT[:].rearrange("t (b c) -> t b c", b=2), att[:, 2:4, :],
                                     ACT.Copy).then_inc(probsT_saved, 1)

            def exponentials(n, p):
                act.wait_ge(shifted_done, n + p + 1)
                nc.scalar.activation(probs[:, p % 2, :], probs[:, p % 2, :], ACT.Exp,
                                     scale=SCALE).then_inc(exp_done, 1)

            def split_y(n, p):
                act.wait_ge(yT_ready, n + p)
                nc.scalar.activation(yT_hi[:].rearrange("p c t -> p (c t)"), att[:, 0, :], ACT.Copy).then_inc(yT_hi_done, 1)

            def split_weights(layer, part):
                act.wait_ge(w_loaded[part], (16 if part == 3 else 64) * (layer + 1))
                nc.scalar.activation(w_hi[:, :, part_columns(part)], raw_weights(layer, part), ACT.Copy).then_inc(w_hi_done, 1)

            split_x(0, first=True)
            split_weights(0, 0)
            split_weights(0, 1)
            act.wait_ge(bias_loaded, 64)
            for u in range(UNITS):
                if u == UNITS - 1:
                    split_x(PAIRS)
                save(u, 0, 0, 0)
                if u == 0:
                    split_weights(0, 2)
                if u == 2:
                    split_weights(0, 3)
                if u == 7:
                    act.wait_ge(k_zeroed, 1)
                    place_k(0, 0, 0, False)
                    act.wait_ge(v_zeroed, 1)

            def stage(n, par, layer, k):
                product_layer = 1 if k == REFRESH_V else layer
                group, group_par = units_group(n, par, k)
                for p in range(PAIRS):
                    before = not (k == FIRST and p == 0)
                    units = slot_units(k, p)
                    if (k, p) == (REFRESH_PROJ, 1):
                        act.wait_ge(proj_ready, LAYER_PAIRS)
                        split_weights(1, 3)
                    if tail(k, p):
                        save_probsT(n, p)
                    if p < 3:
                        place_k(n, p + 1, par, True)
                    elif k != LAST:
                        place_k(n + PAIRS, 0, 1 - par, True)
                    if tail(k, p):
                        split_y(n, p)
                        exponentials(n, p)
                        if units[2] is not None:
                            save(units[2], group, group_par, product_layer)
                        continue
                    save(units[0], group, group_par, product_layer)
                    if before:
                        save_probsT(n, p)
                    exponentials(n, p)
                    save(units[1], group, group_par, product_layer)
                    if before:
                        split_y(n, p)
                    if (k, p) in REFRESHED:
                        split_weights(1, REFRESHED[k, p])
                    if p == 3:
                        split_x(n + 2 * PAIRS)
                    if units[2] is not None:
                        save(units[2], group, group_par, product_layer)

            stages(act, stage)
            save_probsT(ALL_PAIRS, 0)
            split_y(ALL_PAIRS, 0)

        @block.vector
        def _(dve):
            def by_head(ap):
                return ap.unsqueeze(2).broadcast_to([P, HEADS, NODES])

            def transpose_x(n):
                dve.wait_ge(x_in_loaded, 16 * (n + PAIRS))
                for ft in range(KT):
                    nc.vector.transpose(xT[:, ft, :].rearrange("p (b t) -> p b t", t=SQ),
                                        x_in[:, :, SQ * ft:SQ * (ft + 1)]).then_inc(xT_ready, 1)

            def split_x(n):
                for ft in range(KT):
                    dve.wait_ge(xT_hi_done, n + ft + 1)
                    nc.vector.tensor_tensor(xT_lo[:, ft, :], xT[:, ft, :], xT_hi[:, ft, :].bitcast(F32),
                                            ALU.subtract).then_inc(xT_lo_done, 1)

            def shift_scores(n, p):
                heads = probs[:, p % 2, :].rearrange("t (h m) -> t h m", h=HEADS)
                dve.wait_ge(scores_ready, n + p + 1)
                nc.vector.tensor_tensor(
                    heads, att[:, 0:2, :].rearrange("t g (h m) -> t (g h) m", m=NODES),
                    mask[:].unsqueeze(1).broadcast_to([P, HEADS, NODES]), ALU.add).then_inc(masked_done, 1)
                dve.wait_ge(masked_done, n + p + 1)
                nc.vector.tensor_reduce(row_max[:], heads, AX_X, ALU.max).then_inc(max_done, 1)
                dve.wait_ge(max_done, n + p + 1)
                nc.vector.tensor_tensor(heads, heads, by_head(row_max[:]), ALU.subtract).then_inc(shifted_done, 1)

            def sum_probs(n, p):
                heads = probs[:, p % 2, :].rearrange("t (h m) -> t h m", h=HEADS)
                dve.wait_ge(exp_done, n + p + 1)
                nc.vector.tensor_reduce(row_sum[:], heads, AX_X, ALU.add).then_inc(sum_done, 1)
                dve.wait_ge(sum_done, n + p + 1)
                nc.vector.reciprocal(row_inv[:], row_sum[:]).then_inc(inv_done, 1)

            def normalise_probs(n, p):
                heads = probs[:, p % 2, :].rearrange("t (h m) -> t h m", h=HEADS)
                dve.wait_ge(inv_done, n + p + 1)
                nc.vector.tensor_tensor(heads, heads, by_head(row_inv[:]), ALU.mult).then_inc(probs_done, 1)

            def split_y(n, p):
                dve.wait_ge(yT_hi_done, n + p)
                nc.vector.tensor_tensor(yT_lo[:].rearrange("p c t -> p (c t)"), att[:, 0, :],
                                        yT_hi[:].bitcast(F32).rearrange("p c t -> p (c t)"),
                                        ALU.subtract).then_inc(yT_lo_done, 1)

            def residual(n, p):
                q = (p + 3) % 4
                dve.wait_ge(proj_ready, n + p)
                dve.wait_ge(x_res_done, n + p)
                nc.vector.tensor_tensor(x_res[:, q, :], acc[:, 3, :], x_res[:, q, :],
                                        ALU.add).then_inc(residual_done, 1)
                dve.wait_ge(residual_done, n + p)
                nc.vector.bn_stats(stats[:], x_res[:, q, :]).then_inc(stats_done, 1)
                dve.wait_ge(stats_done, n + p).then_inc(aggregate_begun, 1)
                nc.vector.bn_aggr(mean_var[:, q % 2, :], stats[:]).then_inc(mean_var_done, 1)

            def normalise(n, p):
                q = (p + 2) % 4
                dve.wait_ge(rstd_done, n + p - 1)
                nc.vector.tensor_scalar(x_res[:, q, :], x_res[:, q, :], mean_var[:, q % 2, 0:1],
                                        rstd[:, q % 2:q % 2 + 1], ALU.subtract, ALU.mult).then_inc(normed_done, 1)

            def split_weights(layer, part):
                dve.wait_ge(w_hi_done, PARTS * layer + part + 1)
                cols = part_columns(part)
                nc.vector.tensor_tensor(w_lo[:, :, cols], raw_weights(layer, part), w_hi[:, :, cols].bitcast(F32),
                                        ALU.subtract).then_inc(w_lo_done, 1)

            def widen_bias(layer):
                nc.vector.tensor_copy(bias_v_wide, bias_qkv[:, layer, 8:12].unsqueeze(2)
                                      .broadcast_to([P, KT, P])).then_inc(wide_done, 1)

            def finish_bias(layer, bank):
                dve.wait_ge(bias_mixed, layer + 1)
                nc.vector.tensor_tensor(bias_out[:, layer, :], bank, bias_out[:, layer, :], ALU.add).then_inc(bias_out_done, 1)

            transpose_x(0)
            split_x(0)
            split_weights(0, 0)
            split_weights(0, 1)
            dve.wait_ge(adj_loaded, 32)
            dve.wait_ge(consts_done, 5)
            nc.vector.tensor_tensor(mask[:], adj_in[:], eye[:], ALU.add).then_inc(setup, 1)
            dve.wait_ge(setup, 1)
            nc.vector.tensor_scalar(mask[:], mask[:], 0.0, 1.0, ALU.is_gt, ALU.subtract).then_inc(setup, 1)
            dve.wait_ge(setup, 2)
            nc.vector.tensor_scalar(mask[:], mask[:], -MASKED, None, ALU.mult).then_inc(setup, 1)
            dve.wait_ge(setup, 3)
            dve.wait_ge(bias_loaded, 64)
            widen_bias(0)
            split_weights(0, 2)
            split_weights(0, 3)
            finish_bias(0, acc[:, 3, :])
            transpose_x(PAIRS)
            split_x(PAIRS)

            def stage(n, par, layer, k):
                for p in range(PAIRS):
                    shift_scores(n, p)
                    if (k, p) == (REFRESH_PROJ, 1):
                        split_weights(1, 3)
                    if not (k == FIRST and p < 2):
                        normalise(n, p)
                    next_x = p == 3 and k not in (LAST - 1, LAST)
                    if next_x:
                        transpose_x(n + 2 * PAIRS)
                    if not tail(k, p):
                        sum_probs(n, p)
                    if not (k == FIRST and p == 0):
                        split_y(n, p)
                    if tail(k, p):
                        sum_probs(n, p)
                    normalise_probs(n, p)
                    if next_x:
                        split_x(n + 2 * PAIRS)
                    if (k, p) == (REFRESH_V, 1):
                        finish_bias(1, att[:, 2, :])
                    if not (k == FIRST and p == 0):
                        residual(n, p)
                    if (k, p) in REFRESHED:
                        split_weights(1, REFRESHED[k, p])
                    if (k, p) == (REFRESH_V, 0):
                        widen_bias(1)

            stages(dve, stage)
            normalise(ALL_PAIRS, 0)
            split_y(ALL_PAIRS, 0)
            residual(ALL_PAIRS, 0)
            normalise(ALL_PAIRS, 1)

        @block.gpsimd
        def _(pool):
            nc.gpsimd.memset(ident[:], 0.0).then_inc(zeroed, 1)
            nc.gpsimd.memset(eye[:], 0.0).then_inc(zeroed, 1)
            nc.gpsimd.memset(k_diag[:], 0.0).then_inc(k_zeroed, 1)
            nc.gpsimd.memset(minus_half[:], -0.5).then_inc(consts_done, 1)
            nc.gpsimd.memset(epsilon[:], EPS).then_inc(consts_done, 1)
            pool.wait_ge(zeroed, 2)
            nc.gpsimd.affine_select(out=ident[:], in_=ident[:], compare_op=ALU.not_equal, fill=1.0, base=0,
                                    pattern=[[-1, P]], channel_multiplier=1).then_inc(consts_done, 1)
            nc.gpsimd.affine_select(out=eye[:], in_=eye[:], compare_op=ALU.not_equal, fill=1.0, base=0,
                                    pattern=[[-1, NODES]], channel_multiplier=1).then_inc(consts_done, 1)
            pool.wait_ge(consts_done, 4)
            nc.gpsimd.affine_select(out=eye[:], in_=eye[:], compare_op=ALU.not_equal, fill=1.0, base=-NODES,
                                    pattern=[[-1, NODES]], channel_multiplier=1).then_inc(consts_done, 1)
            nc.gpsimd.memset(v_diag[:], 0.0).then_inc(v_zeroed, 1)

            def add_bias(n, p, layer):
                pool.wait_ge(x_res_loaded[p], 4 * n + 16)
                nc.gpsimd.tensor_tensor(x_res[:, p, :], x_res[:, p, :], bias_out[:, layer, :], ALU.add).then_inc(x_res_done, 1)

            def inverse_deviation(n, p):
                q = (p + 3) % 2
                pool.wait_ge(mean_var_done, n + p)
                nc.gpsimd.tensor_tensor(var_eps[:], mean_var[:, q, 1:2], epsilon[:], ALU.add).then_inc(var_eps_done, 1)
                pool.wait_ge(var_eps_done, n + p)
                nc.gpsimd.tensor_tensor(rstd[:, q:q + 1], var_eps[:], minus_half[:], ALU.pow).then_inc(rstd_done, 1)

            def stage(n, par, layer, k):
                for p in range(PAIRS):
                    if k in (FIRST, REFRESH_PROJ) and p == 0:
                        pool.wait_ge(bias_out_done, layer + 1)
                    add_bias(n, p, layer)
                    if not (k == FIRST and p == 0):
                        inverse_deviation(n, p)

            stages(pool, stage)
            inverse_deviation(ALL_PAIRS, 0)


_WEIGHTS = ["Wqkv", "bqkv", "Wproj", "bproj"]


def kernel(**inputs):
    import numpy as _np
    import concourse.bacc as _bacc
    from concourse import mybir as _mybir
    from concourse.bass_utils import run_bass_kernel_spmd as _run

    nc = _bacc.Bacc("TRN2", target_bir_lowering=False, num_devices=1)
    arrays = {}

    def given(name, shape=None):
        a = _np.asarray(inputs[name])
        a = a.reshape(shape) if shape else a
        if name.endswith("bqkv"):
            a = a.reshape(-1, P).T
        a = _np.ascontiguousarray(a)
        arrays[f"in_{name}"] = a
        return nc.dram_tensor(f"in_{name}", a.shape, _mybir.dt.from_np(a.dtype), kind="ExternalInput").ap()

    x = given("x", (TOKENS, E))
    adj = given("adj")
    weights = [[given(f"L{layer}_gnn_{w}") for w in _WEIGHTS] for layer in range(2)]
    out = nc.dram_tensor("out", (TOKENS, E), F32, kind="ExternalOutput").ap()
    build(nc, x, adj, weights, out)
    r = _run(nc, [arrays], core_ids=[0])
    return _np.asarray(r.results[0]["out"]).reshape(inputs["x"].shape)
```
